# Optimizing a Trainium2 kernel written in Bass

```python
import numpy as np
import jax
import jax.numpy as jnp

def _softmax(x, axis=-1):
    return jax.nn.softmax(x, axis=axis)

def _gelu(x):
    return jax.nn.gelu(x, approximate=True)

def _silu(x):
    return jax.nn.silu(x)

def _sigmoid(x):
    return jax.nn.sigmoid(x)

def _layernorm(x, axis=-1, eps=1e-05):
    m = jnp.mean(x, axis=axis, keepdims=True)
    v = jnp.var(x, axis=axis, keepdims=True)
    return (x - m) / jnp.sqrt(v + eps)

def _scatter_add(tgt, idx, src, axis=0):
    return tgt.at[idx].add(src)

def _segment_sum(src, seg, n):
    return jax.ops.segment_sum(src, seg, n)
kernel_name = 'mk_adj_resnorm_d4_adj_r2_275dcd'

def setup_inputs(seed: int=0):
    np.random.seed(seed)
    _w = jnp.asarray

    def _rec_inputs():
        import jax
        import jax.numpy as jnp
        _gk = jax.random.key(seed)
        x = -0.0002928 + 1 * jax.random.normal(jax.random.fold_in(_gk, 1), (2048, 256), jnp.float32)
        _w = (1.0 + jnp.arange(2048, dtype=jnp.float32)) ** (-0.5)
        _w = _w / _w.mean()
        _pij = jnp.clip(0.00195312 * _w[:, None] * _w[None, :], 0.0, 1.0)
        _a = jax.random.uniform(jax.random.fold_in(_gk, 2), (2048, 2048)) < _pij
        _af = _a.astype(jnp.float32)
        adj = _af
        return (x, adj)
    x, adj = _rec_inputs()

    def _L0_gnn_setup():
        import jax, jax.numpy as jnp
        import numpy as np
        N = 4096
        D_IN = 256
        D_OUT = 256
        NEG_BIG = -9000000000000000.0
        key = jax.random.key(seed)
        kx, ka, kw, kb, kn, ke = jax.random.split(key, 6)
        x = jax.random.normal(kx, (N, D_IN), dtype=jnp.float32)
        adj = (jax.random.uniform(ka, (N, N)) > 0.9).astype(jnp.float32)
        stdv = 1.0 / np.sqrt(D_OUT)
        weight = jax.random.uniform(kw, (D_IN, D_OUT), minval=-stdv, maxval=stdv, dtype=jnp.float32)
        bias = jax.random.uniform(kb, (D_OUT,), minval=-stdv, maxval=stdv, dtype=jnp.float32)
        node_w = jax.random.uniform(kn, (D_IN, 1), minval=-1.0, maxval=1.0, dtype=jnp.float32)
        stdv_e = 1.0 / np.sqrt(D_IN)
        edge_w = jax.random.uniform(ke, (D_IN, D_IN), minval=-stdv_e, maxval=stdv_e, dtype=jnp.float32)
        return {'x': x, 'adj': adj, 'weight': weight, 'bias': bias, 'node_w': node_w, 'edge_w': edge_w}
    _L0_gnn_all = _L0_gnn_setup()
    _L0_gnn_in = {k: v for k, v in _L0_gnn_all.items() if k in ('weight', 'bias', 'node_w', 'edge_w')}
    del _L0_gnn_all

    def _L1_gnn_setup():
        import jax, jax.numpy as jnp
        import numpy as np
        N = 3072
        D_IN = 256
        D_OUT = 256
        DENSITY = 0.005
        key = jax.random.key(seed)
        ks = jax.random.split(key, 12)
        x = jax.random.normal(ks[0], (N, D_IN), dtype=jnp.float32)
        adj_a = (jax.random.uniform(ks[1], (N, N)) < DENSITY).astype(jnp.float32)
        adj_b = (jax.random.uniform(ks[2], (N, N)) < DENSITY).astype(jnp.float32)
        W_sa = jax.random.normal(ks[3], (D_IN, D_OUT), dtype=jnp.float32) * (1.414 / np.sqrt(D_IN + D_OUT))
        a_sa = jax.random.normal(ks[4], (1, 2 * D_OUT), dtype=jnp.float32) * (1.414 / np.sqrt(1 + 2 * D_OUT))
        stdv = 1.0 / np.sqrt(D_OUT)
        W_gcnb = jax.random.uniform(ks[5], (D_IN, D_OUT), minval=-stdv, maxval=stdv, dtype=jnp.float32)
        b_gcnb = jax.random.uniform(ks[6], (D_OUT,), minval=-stdv, maxval=stdv, dtype=jnp.float32)
        s = 1.0 / np.sqrt(2 * D_IN)
        Wa = jax.random.uniform(ks[7], (1, 2 * D_IN), minval=-s, maxval=s, dtype=jnp.float32)
        ba = jax.random.uniform(ks[8], (1,), minval=-s, maxval=s, dtype=jnp.float32)
        Wb = jax.random.uniform(ks[9], (1, 2 * D_IN), minval=-s, maxval=s, dtype=jnp.float32)
        bb = jax.random.uniform(ks[10], (1,), minval=-s, maxval=s, dtype=jnp.float32)
        return {'x': x, 'adj_a': adj_a, 'adj_b': adj_b, 'W_sa': W_sa, 'a_sa': a_sa, 'W_gcnb': W_gcnb, 'b_gcnb': b_gcnb, 'Wa': Wa, 'ba': ba, 'Wb': Wb, 'bb': bb}
    _L1_gnn_all = _L1_gnn_setup()
    _L1_gnn_in = {k: v for k, v in _L1_gnn_all.items() if k in ('W_sa', 'a_sa', 'W_gcnb', 'b_gcnb', 'Wa', 'ba', 'Wb', 'bb')}
    del _L1_gnn_all

    def _L2_gnn_setup():
        import jax, jax.numpy as jnp
        import numpy as np
        N = 4096
        IN_F = 256
        OUT_F = 256
        key = jax.random.key(seed)
        k_x, k_adj, k_w = jax.random.split(key, 3)
        x = jax.random.normal(k_x, (N, IN_F), dtype=jnp.float32)
        adj = jax.random.uniform(k_adj, (N, N), dtype=jnp.float32)
        stdv = 1.0 / np.sqrt(OUT_F)
        weight = jax.random.uniform(k_w, (IN_F, OUT_F), dtype=jnp.float32, minval=-stdv, maxval=stdv)
        return {'x': x, 'adj': adj, 'weight': weight}
    _L2_gnn_all = _L2_gnn_setup()
    _L2_gnn_in = {k: v for k, v in _L2_gnn_all.items() if k in ('weight',)}
    del _L2_gnn_all

    def _L3_gnn_setup():
        import jax, jax.numpy as jnp
        import numpy as np
        N, NFEAT, NHID = (4096, 256, 512)

        def _gc(x, adj, W, b):
            return adj @ (x @ W) + b
        key = jax.random.key(seed)
        ks = jax.random.split(key, 8)

        def glorot(k, shape):
            bound = 1.0 / np.sqrt(shape[0])
            return jax.random.uniform(k, shape, jnp.float32, -bound, bound)
        return {'x': jax.random.normal(ks[0], (N, NFEAT), jnp.float32), 'adj': jax.random.uniform(ks[1], (N, N), jnp.float32), 'W1': glorot(ks[2], (NFEAT, NHID)), 'b1': glorot(ks[3], (NHID,)), 'W2': glorot(ks[4], (NHID, NHID)), 'b2': glorot(ks[5], (NHID,)), 'W3': glorot(ks[6], (NHID, NFEAT)), 'b3': glorot(ks[7], (NFEAT,))}
    _L3_gnn_all = _L3_gnn_setup()
    _L3_gnn_in = {k: v for k, v in _L3_gnn_all.items() if k in ('W1', 'b1', 'W2', 'b2', 'W3', 'b3')}
    del _L3_gnn_all
    return {'x': x, 'adj': adj, 'L0_gnn_weight': _L0_gnn_in['weight'], 'L0_gnn_bias': _L0_gnn_in['bias'], 'L0_gnn_node_w': _L0_gnn_in['node_w'], 'L0_gnn_edge_w': _L0_gnn_in['edge_w'], 'L1_gnn_W_sa': _L1_gnn_in['W_sa'], 'L1_gnn_a_sa': _L1_gnn_in['a_sa'], 'L1_gnn_W_gcnb': _L1_gnn_in['W_gcnb'], 'L1_gnn_b_gcnb': _L1_gnn_in['b_gcnb'], 'L1_gnn_Wa': _L1_gnn_in['Wa'], 'L1_gnn_ba': _L1_gnn_in['ba'], 'L1_gnn_Wb': _L1_gnn_in['Wb'], 'L1_gnn_bb': _L1_gnn_in['bb'], 'L2_gnn_weight': _L2_gnn_in['weight'], 'L3_gnn_W1': _L3_gnn_in['W1'], 'L3_gnn_b1': _L3_gnn_in['b1'], 'L3_gnn_W2': _L3_gnn_in['W2'], 'L3_gnn_b2': _L3_gnn_in['b2'], 'L3_gnn_W3': _L3_gnn_in['W3'], 'L3_gnn_b3': _L3_gnn_in['b3']}

def reference(x, adj, L0_gnn_weight, L0_gnn_bias, L0_gnn_node_w, L0_gnn_edge_w, L1_gnn_W_sa, L1_gnn_a_sa, L1_gnn_W_gcnb, L1_gnn_b_gcnb, L1_gnn_Wa, L1_gnn_ba, L1_gnn_Wb, L1_gnn_bb, L2_gnn_weight, L3_gnn_W1, L3_gnn_b1, L3_gnn_W2, L3_gnn_b2, L3_gnn_W3, L3_gnn_b3):
    import jax
    import jax.numpy as jnp

    def _L0_gnn_ref(x, adj, weight, bias, node_w, edge_w):
        import jax, jax.numpy as jnp
        import numpy as np
        N = 4096
        D_IN = 256
        D_OUT = 256
        NEG_BIG = -9000000000000000.0
        node_att = jax.nn.softmax(x @ node_w, axis=0)
        h = x @ edge_w
        e = h @ h.T
        e = jnp.where(adj > 0, e, NEG_BIG)
        edge_att = jax.nn.softmax(e, axis=1)
        combined_att = node_att * edge_att
        support = x @ weight
        output = adj * combined_att @ support
        return output + bias

    def _L1_gnn_ref(x, adj_a, adj_b, W_sa, a_sa, W_gcnb, b_gcnb, Wa, ba, Wb, bb):
        import jax, jax.numpy as jnp
        import numpy as np
        N = 3072
        D_IN = 256
        D_OUT = 256
        DENSITY = 0.005
        type_sum_a = adj_a @ x
        type_sum_b = adj_b @ x
        attn_a = jax.nn.sigmoid(jnp.concatenate([type_sum_a, x], axis=1) @ Wa.T + ba)
        attn_b = jax.nn.sigmoid(jnp.concatenate([type_sum_b, x], axis=1) @ Wb.T + bb)
        h = x @ W_sa
        Hd = h.shape[1]
        s_left = h @ a_sa[0, :Hd]
        s_right = h @ a_sa[0, Hd:]
        scores = s_left[:, None] + s_right[None, :]
        e = jnp.where(adj_a != 0, jnp.exp(-jax.nn.leaky_relu(scores, 0.01)), 0.0)
        attn = e / (jnp.sum(e, axis=1, keepdims=True) + 1e-05)
        x_a = attn @ h
        x_b = adj_b @ (x @ W_gcnb) + b_gcnb
        return jax.nn.sigmoid(attn_a * x_a + attn_b * x_b)

    def _L2_gnn_ref(x, adj, weight):
        import jax, jax.numpy as jnp
        import numpy as np
        N = 4096
        IN_F = 256
        OUT_F = 256
        n = adj.shape[0]
        adj_hat = adj + jnp.eye(n, dtype=adj.dtype)
        rowsum = adj_hat.sum(axis=1)
        d_inv_sqrt = jnp.power(rowsum, -0.5)
        d_inv_sqrt = jnp.where(jnp.isinf(d_inv_sqrt), 0.0, d_inv_sqrt)
        adj_norm = adj_hat * d_inv_sqrt[:, None] * d_inv_sqrt[None, :]
        support = x @ weight
        out = adj_norm @ support
        return jax.nn.relu(out)

    def _L3_gnn_ref(x, adj, W1, b1, W2, b2, W3, b3):
        import jax, jax.numpy as jnp
        import numpy as np
        N, NFEAT, NHID = (4096, 256, 512)

        def _gc(x, adj, W, b):
            return adj @ (x @ W) + b
        h = jax.nn.relu(_gc(x, adj, W1, b1))
        h = jax.nn.relu(_gc(h, adj, W2, b2))
        return _gc(h, adj, W3, b3)
    x = _layernorm(x + _L0_gnn_ref(x, adj, L0_gnn_weight, L0_gnn_bias, L0_gnn_node_w, L0_gnn_edge_w), axis=-1)
    x = _layernorm(x + _L1_gnn_ref(x, adj, adj, L1_gnn_W_sa, L1_gnn_a_sa, L1_gnn_W_gcnb, L1_gnn_b_gcnb, L1_gnn_Wa, L1_gnn_ba, L1_gnn_Wb, L1_gnn_bb), axis=-1)
    x = _layernorm(x + _L2_gnn_ref(x, adj, L2_gnn_weight), axis=-1)
    x = _layernorm(x + _L3_gnn_ref(x, adj, L3_gnn_W1, L3_gnn_b1, L3_gnn_W2, L3_gnn_b2, L3_gnn_W3, L3_gnn_b3), axis=-1)
    return x

_drawn_inputs = setup_inputs


def setup_inputs(seed=0):
    import zlib

    import numpy as np

    out = dict(_drawn_inputs(seed))
    spreads = {}
    factors = {'L0_gnn_weight': 64.0,
     'L0_gnn_node_w': 53.394,
     'L0_gnn_edge_w': 64.0,
     'L1_gnn_a_sa': 4.119,
     'L1_gnn_b_gcnb': 4.44,
     'L1_gnn_Wa': 3.806,
     'L3_gnn_b1': 3.803,
     'L3_gnn_b2': 5.655,
     'L3_gnn_b3': 3.177}
    for name, (base, spread) in spreads.items():
        noise = np.random.default_rng([zlib.crc32(name.encode()), seed]).standard_normal(out[name].shape)
        drawn = base * np.exp(spread * noise) if base else spread * noise
        out[name] = jnp.asarray(drawn.astype(out[name].dtype))
    for name, factor in factors.items():
        out[name] = (out[name] * factor).astype(out[name].dtype)
    return out
```

```python
from contextlib import ExitStack

import numpy as np
import concourse.bass as bass
from concourse import mybir

F32 = mybir.dt.float32
F32R = mybir.dt.float32r
BF16 = mybir.dt.bfloat16
F16 = mybir.dt.float16
ALU = mybir.AluOpType
ACT = mybir.ActivationFunctionType
AX_X = mybir.AxisListType.X
RMAX = bass.bass_isa.ReduceOp.max
RADD = bass.bass_isa.ReduceOp.add
HI, LO = 0, 1


class Chain:

    def __init__(self, eng, sem):
        self.eng, self.sem, self.base, self.n = eng, sem, 0, 0

    def link(self, ins):
        ins.then_inc(self.sem, 1)
        self.n += 1
        self.eng.wait_ge(self.sem, self.base + self.n)

    def enter(self, i, per_round):
        self.start, self.per_round = self.base + self.n, per_round
        self.base, self.n = i * per_round + self.start, 0

    def leave(self, rounds):
        assert self.n == self.per_round, (self.n, self.per_round)
        self.base, self.n = self.start + rounds * self.per_round, 0


def wait_from(eng, sem, value):
    if not isinstance(value, int) or value > 0:
        eng.wait_ge(sem, value)


def pause(eng, turns):
    eng.sem_inc(turns, 1)


def tile(tensor, t):
    return tensor[:, bass.ds(t, 1), :].rearrange("p a d -> p (a d)")


def build(nc, x_in, adj_in, w0_in, b0_in, node_in, edge_in, wsa_in, asa_in, wg_in, bg_in,
          wa_in, ba_in, wb_in, bb_in, wl2_in, W1_in, b1_in, W2_in, b2_in, W3_in, b3_in, out):
    N, D = x_in.shape
    HID = W1_in.shape[1]
    P = 128
    T = N // P
    KD = D // P
    KH = HID // P
    CB = 512
    B = N // CB
    TB = CB // P
    HALF = N // 2
    BIG = 9.0e15
    FAR = 1.0e38
    EPS = 1e-5
    SLOPE = 0.01
    XS = 2048.0
    TOP = 16384.0
    RE = 4
    AHEAD = 3
    P0_GROUPS = 2 * KD * B + T
    P1_SPLITS = KD * B + T
    P1_GROUPS = P1_SPLITS + B
    assert HID == CB and N == 2 * 8 * P

    def w_tiles(w):
        return w.rearrange("(k p) n -> p k n", p=P)

    def vec_row(v):
        return v.rearrange("(a n) -> a n", a=1).to_broadcast([P, v.shape[0]])

    ctx = ExitStack()
    with ctx:
        def sb(stack, name, shape, dt=F32):
            return stack.enter_context(nc.sbuf_tensor(name, shape, dt))

        def pair(stack, name, shape, dt=F32R):
            return [sb(stack, name + n, shape, dt) for n in ("_hi", "_lo")]

        def sem(name):
            return ctx.enter_context(nc.semaphore(name))

        adjT = sb(ctx, "adjT", [P, T, N], BF16)
        x = sb(ctx, "x", [P, T, D])
        ident = sb(ctx, "ident", [P, P])
        identb = sb(ctx, "identb", [P, P], BF16)
        deg = sb(ctx, "deg", [P, T, 2])
        dinv = sb(ctx, "dinv", [P, T])
        dsc = sb(ctx, "dsc", [P, T])
        ones = sb(ctx, "ones", [P, T])
        epsc = sb(ctx, "epsc", [P, 1])
        mhalf = sb(ctx, "mhalf", [P, T])
        stats = sb(ctx, "stats", [P, 2, 6])
        mv = sb(ctx, "mv", [P, 2, 2])
        rstd = sb(ctx, "rstd", [P, 2, 2])
        y = sb(ctx, "y", [P, 2, D])
        xb = sb(ctx, "xb", [P, 2, D])
        brow = sb(ctx, "brow", [P, D])
        gm = sb(ctx, "gm", [P, T])
        g1 = sb(ctx, "g1", [P, 4])

        lay0 = ExitStack()
        hT = pair(lay0, "hT", [P, KD, N])
        sup = sb(lay0, "sup", [P, T, 2 * D], F32R)
        nl = sb(lay0, "nl", [P, T])
        nst = sb(lay0, "nst", [P, 5])
        pre0 = ExitStack()
        w0x = sb(pre0, "w0x", [P, KD, D + 2])
        we = sb(pre0, "we", [P, KD, D])
        w0s = pair(pre0, "w0s", [P, KD, D + 2])
        wes = pair(pre0, "wes", [P, KD, D])
        xT0 = pair(pre0, "xT0", [P, KD, N])
        pre0.close()
        main0 = ExitStack()
        em = sb(main0, "em", [P, 2, N])
        PT = pair(main0, "PT", [P, T, P])
        adjf = sb(main0, "adjf", [P, 2, HALF])
        adjb = sb(main0, "adjb", [P, N], BF16)
        fill = sb(main0, "fill", [P, N], BF16)
        hst = pair(main0, "hst", [P, 2, KD, P])
        mx = sb(main0, "mx", [P, 2, 2])
        negm = sb(main0, "negm", [P, 2])
        Z = sb(main0, "Z", [P, 2])
        rowf = sb(main0, "rowf", [P, 2, 3])
        main0.close()
        lay0.close()

        lay123 = ExitStack()
        x16 = sb(lay123, "x16", [P, 2, T, D], F16)
        agg = pair(lay123, "agg", [P, KD, CB])
        lay1 = ExitStack()
        H = pair(lay1, "H", [P, T, D + 2])
        slrow = sb(lay1, "slrow", [P, N])
        ex = sb(lay1, "ex", [P, T, 4])
        vj = sb(lay1, "vj", [P, T, 1])
        wi = sb(lay1, "wi", [P, T])
        bab = sb(lay1, "bab", [P, 1, 2])
        wgs = pair(lay1, "wgs", [P, KD, D + 2])
        pre1 = ExitStack()
        wsx = sb(pre1, "wsx", [P, KD, D + 4])
        wss = pair(pre1, "wss", [P, KD, D + 4])
        wlb = pair(pre1, "wlb", [P, KD, P])
        wgx = sb(pre1, "wgx", [P, KD, D + 2])
        arow = sb(pre1, "arow", [P, 2 * D])
        scr = sb(pre1, "scr", [P, D])
        xT1 = pair(pre1, "xT1", [P, KD, N])
        pre1.close()
        main1 = ExitStack()
        nb = sb(main1, "nb", [P, 2, CB], BF16)
        tm = sb(main1, "tm", [P, 2, CB])
        ef = sb(main1, "ef", [P, RE, CB])
        es = pair(main1, "es", [P, RE, CB])
        g4 = sb(main1, "g4", [P, TB, D])
        gate = sb(main1, "gate", [P, TB, 2])
        rz = sb(main1, "rz", [P, TB])
        z1 = sb(main1, "z1", [P, 2, D])
        main1.close()
        lay1.close()
        lay23 = ExitStack()
        hf = sb(lay23, "hf", [P, 2, CB])
        hh = pair(lay23, "hh", [P, KH, CB])
        b1c = sb(lay23, "b1c", [P, KH])
        b2c = sb(lay23, "b2c", [P, KH])
        w12 = ExitStack()
        W1s = pair(w12, "W1s", [P, KD, HID])
        W2s = pair(w12, "W2s", [P, KH, HID])
        W1f = sb(w12, "W1f", [P, KD, HID])
        W2f = sb(w12, "W2f", [P, KH, HID])
        w12.close()
        w3 = ExitStack()
        W3f = sb(w3, "W3f", [P, KH, D])
        W3s = pair(w3, "W3s", [P, KH, D])
        F = sb(w3, "F", [P, T, D])
        ob = sb(w3, "ob", [P, 2, D])
        w3.close()
        used = 2 * (KD + KH) * HID * 4 + (KD + KH) * HID * 4
        gap = sb(lay23, "gap", [P, used // 4])
        wl2 = ExitStack()
        wlf = sb(wl2, "wlf", [P, KD, D])
        wls = pair(wl2, "wls", [P, KD, D])
        wl2.close()
        G = sb(lay23, "G", [P, T + AHEAD, HID])
        lay23.close()
        lay123.close()

        ps = ctx.enter_context(nc.psum_tensor("ps", [P, 8, CB], F32))

        def bank(n, cols=CB):
            return ps[:, n, 0:cols]

        def g16(t, part, c0=0, cols=HID):
            return G[:, t, :].bitcast(F16)[:, part * HID + c0:part * HID + c0 + cols]

        f16 = x16[:, :, :, :].rearrange("p a t d -> p (a t d)").rearrange("p (t c) -> p t c", t=T)

        x_landed = [sem(f"x_landed{c}") for c in range(B)]
        w0_landed, adj_landed = sem("w0_landed"), [sem(f"adj_landed{k}") for k in range(2)]
        wt1_landed, wt2_landed = sem("wt1_landed"), sem("wt2_landed")
        wh_landed, w3_landed = sem("wh_landed"), sem("w3_landed")
        const_ready = sem("const_ready")
        w_ready = sem("w_ready")
        wp_ready = sem("wp_ready")
        p0_mm, p0_hi, p0_lo = sem("p0_mm"), sem("p0_hi"), sem("p0_lo")
        node_max, node_gmax, node_neg = sem("node_max"), sem("node_gmax"), sem("node_neg")
        node_exp, node_sum = sem("node_exp"), sem("node_sum")
        h_staged, e_mm, e_read, e_maxed = sem("h_staged"), sem("e_mm"), sem("e_read"), sem("e_maxed")
        adj_cast, adj_tr, adj_ev = sem("adj_cast"), sem("adj_tr"), [sem(f"adj_ev{k}") for k in range(2)]
        fill_ready, exp_done = sem("fill_ready"), sem("exp_done")
        pt_tr, pt_hi, pt_lo = sem("pt_tr"), sem("pt_hi"), sem("pt_lo")
        pv_mm, pv_read, xb_ready, xb_used = sem("pv_mm"), sem("pv_read"), sem("xb_ready"), sem("xb_used")
        y_normed = sem("y_normed")
        var_ready, rstd_ready = sem("var_ready"), sem("rstd_ready")
        turns = sem("turns")
        act_own, dve_own, pool_own = sem("act_own"), sem("dve_own"), sem("pool_own")
        l0_done, l1_done, l2_done = sem("l0_done"), sem("l1_done"), sem("l2_done")
        h1_done, h2_done = sem("h1_done"), sem("h2_done")
        conv_hi, conv_lo = sem("conv_hi"), sem("conv_lo")
        agg_mm, agg_hi, agg_lo = sem("agg_mm"), sem("agg_hi"), sem("agg_lo")
        wlb_ready = sem("wlb_ready")
        p1_mm, p1_hi, p1_lo, ex_ready = sem("p1_mm"), sem("p1_hi"), sem("p1_lo"), sem("ex_ready")
        w_exp, H_ready = sem("w_exp"), sem("H_ready")
        tm_ready, ef_ready, es_hi, es_lo, e_used = (sem("tm_ready"), sem("ef_ready"), sem("es_hi"),
                                                    sem("es_lo"), sem("e_used"))
        g_mm, g_ev, gate_tanh, gate_ready = sem("g_mm"), sem("g_ev"), sem("gate_tanh"), sem("gate_ready")
        z1_ready, z_ready, sig_ready = sem("z1_ready"), sem("z_ready"), sem("sig_ready")
        dinv_ready, dsc_ready = sem("dinv_ready"), sem("dsc_ready")
        o2_mm, relu_ready, y2_ready = sem("o2_mm"), sem("relu_ready"), sem("y2_ready")
        h_mm, h_f, h_hi, h_lo = sem("h_mm"), sem("h_f"), sem("h_hi"), sem("h_lo")
        r_mm, r_copied, r_maxed = sem("r_mm"), sem("r_copied"), sem("r_maxed")
        tmax_ready, gmax_ready, scale_ready = sem("tmax_ready"), sem("gmax_ready"), sem("scale_ready")
        c3_hi, c3_lo = sem("c3_hi"), sem("c3_lo")
        o3_mm, o3_read, o_stored = sem("o3_mm"), sem("o3_read"), [sem(f"o_stored{u}") for u in range(2)]

        CREDITS = {"act": ((h_f, 2), (r_copied, 2), (relu_ready, TB)), "dve": ((h_lo, 2), (y2_ready, 2))}

        block = ctx.enter_context(nc.Block())

        ctx.enter_context(nc.allow_non_contiguous_dma(reason="a few columns of weights and biases"))

        @block.sync
        def _(sp):
            x_tiles = x_in.rearrange("(t p) d -> p t d", p=P)
            for c in range(B):
                sp.dma_start(x[:, TB * c:TB * c + TB, :], x_tiles[:, TB * c:TB * c + TB, :]).then_inc(x_landed[c], 16)
                if c == 0:
                    sp.dma_start(we[:, :, :], w_tiles(edge_in)).then_inc(w0_landed, 16)
                    sp.dma_start(w0x[:, :, 0:D], w_tiles(w0_in)).then_inc(w0_landed, 16)
                    sp.dma_start(w0x[:, :, D:D + 1], w_tiles(node_in)).then_inc(w0_landed, 16)
                    sp.dma_start(brow[:, :], vec_row(b0_in)).then_inc(w0_landed, 16)

            def load_adj(t):
                for k in range(2):
                    wait_from(sp, adj_cast, 2 * (t - 1) + k + 1)
                    sp.dma_start(adjf[:, k, :], adj_in[bass.ds(t * P, P), k * HALF:(k + 1) * HALF]) \
                        .then_inc(adj_landed[k], 16)

            sp.wait_ge(p0_lo, P0_GROUPS)
            load_adj(0)
            with sp.Fori(1, T) as t:
                load_adj(t)

            sp.wait_ge(l0_done, 4)
            sp.dma_start(wsx[:, :, 0:D], w_tiles(wsa_in)).then_inc(wt1_landed, 16)
            sp.dma_start(arow[:, :], asa_in.to_broadcast([P, 2 * D])).then_inc(wt1_landed, 16)
            sp.dma_start(wgx[:, :, 0:D], w_tiles(wg_in)).then_inc(wt1_landed, 16)
            for g, (w, b) in enumerate(((wa_in, ba_in), (wb_in, bb_in))):
                cols = w.rearrange("a (s k p) -> p s k a", s=2, p=P)
                sp.dma_start(wgx[:, :, D + g:D + g + 1], cols[:, 0, :, :]).then_inc(wt1_landed, 16)
                sp.dma_start(wsx[:, :, D + 2 + g:D + 3 + g], cols[:, 1, :, :]).then_inc(wt1_landed, 16)
                sp.dma_start(bab[:, 0, g:g + 1], vec_row(b)).then_inc(wt1_landed, 16)
            sp.dma_start(brow[:, :], vec_row(bg_in)).then_inc(wt1_landed, 16)

            sp.wait_ge(l1_done, 4)
            sp.dma_start(wlf[:, :, :], w_tiles(wl2_in)).then_inc(wt2_landed, 16)
            sp.dma_start(W1f[:, :, :], w_tiles(W1_in)).then_inc(wh_landed, 16)
            sp.dma_start(W2f[:, :, :], w_tiles(W2_in)).then_inc(wh_landed, 16)
            sp.dma_start(b1c[:, :], b1_in.rearrange("(k p) -> p k", p=P)).then_inc(wh_landed, 16)
            sp.dma_start(b2c[:, :], b2_in.rearrange("(k p) -> p k", p=P)).then_inc(wh_landed, 16)
            sp.dma_start(brow[:, :], vec_row(b3_in)).then_inc(wh_landed, 16)
            sp.wait_ge(h1_done, 4)
            sp.dma_start(W3f[:, :, :], w_tiles(W3_in)).then_inc(w3_landed, 16)

            with sp.Fori(0, T // 2) as i:
                for u in range(2):
                    sp.wait_ge(y_normed, 3 * T + 2 * i + u + 1)
                    sp.dma_start(out[bass.ds((2 * i + u) * P, P), :], ob[:, u, :]).then_inc(o_stored[u], 16)
            for u in range(2):
                sp.wait_ge(o_stored[u], 16 * (T // 2))

        @block.gpsimd
        def _(pool):
            own = Chain(pool, pool_own)
            for m in (ident, identb):
                own.link(nc.gpsimd.memset(m[:, :], 0.0))
                nc.gpsimd.affine_select(out=m[:, :], in_=m[:, :], compare_op=ALU.not_equal, fill=1.0, base=0,
                                        pattern=[[-1, P]], channel_multiplier=1).then_inc(const_ready, 1)
            own.link(nc.gpsimd.memset(epsc[:, :], EPS))
            own.link(nc.gpsimd.memset(ones[:, :], 1.0))
            own.link(nc.gpsimd.memset(mhalf[:, :], -0.5))
            nc.gpsimd.memset(w0x[:, :, D + 1:D + 2], 0.0).then_inc(const_ready, 1)

            def norm_factor(m, u):
                pool.wait_ge(var_ready, m + 1)
                own.link(nc.gpsimd.tensor_tensor(rstd[:, u, 0:1], mv[:, u, 1:2], epsc[:, :], ALU.add))
                nc.gpsimd.tensor_tensor(rstd[:, u, 1:2], rstd[:, u, 0:1], mhalf[:, 0:1], ALU.pow) \
                    .then_inc(rstd_ready, 1)

            pool.wait_ge(node_max, 1)
            nc.gpsimd.partition_all_reduce(nst[:, 1:2], nst[:, 0:1], P, RMAX).then_inc(node_gmax, 1)

            def stage_h(t, u):
                wait_from(pool, e_mm, 2 * (t - 1))
                for part in (HI, LO):
                    nc.gpsimd.tensor_copy(hst[part][:, u, :, :],
                                          hT[part][:, :, bass.ds(t * P, P)].bitcast(F32)).then_inc(h_staged, 1)

            def bias_x(t, u, before=0):
                wait_from(pool, xb_used, before + t)
                nc.gpsimd.tensor_tensor(xb[:, u, :], tile(x, t), brow[:, :], ALU.add).then_inc(xb_ready, 1)

            pool.wait_ge(w0_landed, 64)
            for c in range(B):
                pool.wait_ge(x_landed[c], 16)
            pool.wait_ge(p0_lo, P0_GROUPS)
            stage_h(0, 0)
            pool.wait_ge(node_exp, 1)
            nc.gpsimd.partition_all_reduce(nst[:, 4:5], nst[:, 3:4], P, RADD).then_inc(node_sum, 1)
            stage_h(1, 1)
            bias_x(0, 0)
            with pool.Fori(0, T // 2 - 1) as i:
                own.enter(i, 2)
                for u in range(2):
                    stage_h(2 * i + 2 + u, u)
                    bias_x(2 * i + 1 + u, 1 - u)
                    norm_factor(2 * i + u, u)
            own.leave(T // 2 - 1)
            bias_x(T - 1, 1)
            norm_factor(T - 2, 0)
            norm_factor(T - 1, 1)
            pool.drain().then_inc(l0_done, 1)

            pool.wait_ge(l0_done, 4)
            own.link(nc.gpsimd.tensor_tensor(dinv[:, :], deg[:, :, 0], deg[:, :, 1], ALU.add))
            own.link(nc.gpsimd.tensor_tensor(dinv[:, :], dinv[:, :], ones[:, :], ALU.add))
            nc.gpsimd.tensor_tensor(dinv[:, :], dinv[:, :], mhalf[:, :], ALU.pow).then_inc(dinv_ready, 1)
            for t in range(T):
                nc.gpsimd.tensor_scalar(x16[:, HI, t, :], x[:, t, :], XS, None, ALU.mult).then_inc(conv_hi, 1)
            pool.wait_ge(w_ready, 2)
            for part in (HI, LO):
                nc.gpsimd.tensor_copy(wlb[part][:, :, :],
                                      wss[part][:, :, D + 1:D + 2].bitcast(F32).to_broadcast([P, KD, P])) \
                    .then_inc(wlb_ready, 1)

            def exp_parts(b):
                for jt in range(T):
                    n = b * T + jt
                    pool.wait_ge(ef_ready, n + 1)
                    wait_from(pool, e_used, n + 1 - RE)
                    pause(pool, turns)
                    nc.gpsimd.tensor_copy(es[HI][:, jt % RE, :], ef[:, jt % RE, :]).then_inc(es_hi, 1)
                for k in range(TB):
                    norm_factor(T + b * TB + k, k % 2)

            pool.wait_ge(p1_mm, P1_GROUPS)
            exp_parts(0)
            with pool.Fori(1, B) as b:
                own.enter(b - 1, TB)
                exp_parts(b)
            own.leave(B - 1)
            pool.drain().then_inc(l1_done, 1)

            pool.wait_ge(l1_done, 4)
            pool.wait_ge(wh_landed, 80)
            for f, s in ((W1f, W1s), (W2f, W2s)):
                own.link(nc.gpsimd.tensor_copy(s[HI][:, :, :], f[:, :, :]))
                nc.gpsimd.tensor_tensor(s[LO][:, :, :], f[:, :, :], s[HI][:, :, :].bitcast(F32), ALU.subtract) \
                    .then_inc(wp_ready, 1)
            with pool.Fori(0, T // 2) as i:
                own.enter(i, 2)
                for u in range(2):
                    norm_factor(2 * T + 2 * i + u, u)
            own.leave(T // 2)
            pool.drain().then_inc(l2_done, 1)

            def hidden_block(b):
                for o in range(KH):
                    pool.wait_ge(h_f, 2 + b * KH + o + 1)
                    if o == 0:
                        wait_from(pool, r_mm, b * TB)
                    pause(pool, turns)
                    nc.gpsimd.tensor_copy(hh[HI][:, o, :], hf[:, o % 2, :]).then_inc(h_hi, 1)

            pool.wait_ge(l2_done, 4)
            hidden_block(0)
            with pool.Fori(1, B) as b:
                hidden_block(b)
            pool.drain().then_inc(h1_done, 1)
            pool.wait_ge(tmax_ready, 1)
            nc.gpsimd.partition_all_reduce(g1[:, 1:2], g1[:, 0:1], P, RMAX).then_inc(gmax_ready, 1)
            pool.wait_ge(h1_done, 4)
            pool.wait_ge(w3_landed, 16)
            own.link(nc.gpsimd.tensor_copy(W3s[HI][:, :, :], W3f[:, :, :]))
            nc.gpsimd.tensor_tensor(W3s[LO][:, :, :], W3f[:, :, :], W3s[HI][:, :, :].bitcast(F32), ALU.subtract) \
                .then_inc(wp_ready, 1)
            with pool.Fori(B, 2 * B) as b:
                hidden_block(b)
            pool.drain().then_inc(h2_done, 1)
            pool.wait_ge(tmax_ready, 2)
            nc.gpsimd.partition_all_reduce(g1[:, 1:2], g1[:, 0:1], P, RMAX).then_inc(gmax_ready, 1)

            bias_x(0, 0, T)
            bias_x(1, 1, T)
            with pool.Fori(0, T // 2 - 1) as i:
                own.enter(i, 2)
                for u in range(2):
                    norm_factor(3 * T + 2 * i + u, u)
                    bias_x(2 * i + 2 + u, u, T)
            own.leave(T // 2 - 1)
            for u in range(2):
                norm_factor(4 * T - 2 + u, u)

        @block.tensor
        def _(pe):
            mm = nc.tensor.matmul

            def project(to, s, cols, w, width, tiles=None):
                tiles = tiles or range(KD)
                for k in tiles:
                    for a, b in ((HI, HI), (HI, LO), (LO, HI)):
                        ins = mm(to, s[a][:, k, cols], w[b][:, k, 0:width],
                                 start=(k == 0 and (a, b) == (HI, HI)),
                                 stop=(k == tiles[-1] and a == LO))
                return ins

            pe.wait_ge(const_ready, 3)
            for n in range(P0_GROUPS):
                if n >= 4:
                    pe.wait_ge(p0_lo, n - 3)
                to = 4 + n % 4
                if n < 2 * B:
                    b, f = n // KD, n % KD
                    pe.wait_ge(x_landed[b], 16)
                    for k in range(TB):
                        ins = nc.tensor.transpose(ps[:, to, k * P:(k + 1) * P],
                                                  x[:, b * TB + k, f * P:(f + 1) * P], ident[:, :])
                elif n < 4 * B:
                    b, o = (n - 2 * B) // KD, n % KD
                    pe.wait_ge(p0_lo, 2 * (b + 1))
                    if n == 2 * B:
                        pe.wait_ge(w_ready, 1)
                    for k in range(KD):
                        for p, q in ((HI, HI), (HI, LO), (LO, HI)):
                            ins = mm(bank(to), wes[p][:, k, o * P:(o + 1) * P], xT0[q][:, k, b * CB:(b + 1) * CB],
                                     start=(k == 0 and (p, q) == (HI, HI)), stop=(k == KD - 1 and p == LO))
                else:
                    t = n - 4 * B
                    ins = project(bank(to, D + 2), xT0, slice(t * P, (t + 1) * P), w0s, D + 2)
                ins.then_inc(p0_mm, 1)

            def scores(t, u):
                pe.wait_ge(h_staged, 2 * (t + 1))
                for c in range(B):
                    if c % 2 == 0:
                        wait_from(pe, e_read, 2 * (t - 1) + c // 2 + 1)
                    for k in range(KD):
                        for p, q in ((HI, HI), (HI, LO), (LO, HI)):
                            ins = mm(bank(c), hst[p][:, u, k, :], hT[q][:, k, c * CB:(c + 1) * CB],
                                     start=(k == 0 and (p, q) == (HI, HI)), stop=(k == KD - 1 and p == LO))
                    if c % 2:
                        ins.then_inc(e_mm, 1)

            def adj_transpose(t, k):
                pe.wait_ge(adj_cast, 2 * t + k + 1)
                wait_from(pe, adj_ev[1 - k], t + k)
                to = ps[:, 6, :].bitcast(BF16)
                for j in range(T // 2):
                    c = k * HALF + j * P
                    ins = nc.tensor.transpose(to[:, j * P:(j + 1) * P], adjb[:, c:c + P], identb[:, :])
                ins.then_inc(adj_tr, 1)

            def weighted(t, u, between):
                def turn(g):
                    n = t * TB + g
                    if g == 0:
                        pe.wait_ge(exp_done, t + 1)
                    wait_from(pe, pt_lo, n - 1)
                    for j in range(4):
                        jt = 4 * g + j
                        ins = nc.tensor.transpose(ps[:, 4 + g % 2, j * P:(j + 1) * P],
                                                  em[:, u, jt * P:(jt + 1) * P], ident[:, :])
                    ins.then_inc(pt_tr, 1)

                def times(g):
                    pe.wait_ge(pt_lo, t * TB + g + 1)
                    if g == 0:
                        wait_from(pe, pv_read, t)
                    for j in range(4):
                        jt = 4 * g + j
                        for part in ((HI, LO) if jt == 0 else (LO, HI)):
                            if part == HI:
                                ins = mm(bank(7), PT[HI][:, jt, :], sup[:, jt, :], start=(jt == 0),
                                         stop=(jt == T - 1))
                            else:
                                ins = mm(bank(7, D), PT[LO][:, jt, :], sup[:, jt, 0:D], start=False, stop=False,
                                         skip_group_check=True)
                    return ins

                turn(0)
                turn(1)
                times(0)
                turn(2)
                times(1)
                turn(3)
                between()
                times(2)
                times(3).then_inc(pv_mm, 1)

            def round0(t, u):
                scores(t, u)
                adj_transpose(t, 0)
                if isinstance(t, int) and t == 0:
                    adj_transpose(0, 1)
                else:
                    weighted(t - 1, 1 - u, lambda: adj_transpose(t, 1))

            round0(0, 0)
            round0(1, 1)
            with pe.Fori(0, T // 2 - 1) as i:
                for u in range(2):
                    round0(2 * i + 2 + u, u)
            weighted(T - 1, 1, lambda: None)
            pe.drain().then_inc(l0_done, 1)

            pe.wait_ge(l0_done, 4)
            for n in range(P1_GROUPS):
                if n >= 4:
                    pe.wait_ge(p1_hi, n - 3)
                    pe.wait_ge(p1_lo, min(n - 3, P1_SPLITS))
                to = n % 4
                if n < 2 * B:
                    b, f = n // KD, n % KD
                    for k in range(TB):
                        ins = nc.tensor.transpose(ps[:, to, k * P:(k + 1) * P],
                                                  x[:, b * TB + k, f * P:(f + 1) * P], ident[:, :])
                elif n < P1_SPLITS:
                    t = n - 2 * B
                    if t == 0:
                        pe.wait_ge(w_ready, 2)
                        pe.wait_ge(p1_lo, 2 * B)
                    ins = project(bank(to, D + 4), xT1, slice(t * P, (t + 1) * P), wss, D + 4)
                else:
                    b = n - P1_SPLITS
                    if b == 0:
                        pe.wait_ge(wlb_ready, 2)
                    for k in range(KD):
                        for p, q in ((HI, HI), (HI, LO), (LO, HI)):
                            ins = mm(bank(to), wlb[p][:, k, :], xT1[q][:, k, b * CB:(b + 1) * CB],
                                     start=(k == 0 and (p, q) == (HI, HI)), stop=(k == KD - 1 and p == LO))
                ins.then_inc(p1_mm, 1)

            def aggregate(layer, b, f, diag=False):
                wait_from(pe, agg_lo, (layer * B + b) * KD + f - 1)
                for jt in range(T):
                    if f == 0 and isinstance(b, int) and b == 0:
                        pe.wait_ge(conv_lo, layer * T + jt + 1)
                    for part in (HI, LO):
                        ins = mm(bank(4 + f), x16[:, part, jt, f * P:(f + 1) * P],
                                 adjT[:, jt, bass.ds(b * CB, CB)], start=(jt == 0 and part == HI),
                                 stop=(jt == T - 1 and part == LO))
                    if diag and jt == 0:
                        if isinstance(b, int) and b == 0:
                            pe.wait_ge(conv_lo, layer * T + TB)
                        for k in range(TB):
                            for part in (HI, LO):
                                mm(ps[:, 4 + f, k * P:(k + 1) * P],
                                   tile(x16[:, part, :, f * P:(f + 1) * P], b * TB + k),
                                   identb[:, :], start=False, stop=False, skip_group_check=True)
                ins.then_inc(agg_mm, 1)

            def attend(b, jts):
                for jt in jts:
                    pe.wait_ge(es_lo, b * T + jt + 1)
                    if jt == 0:
                        wait_from(pe, z_ready, b * TB)
                    for k in range(TB):
                        for p, q in ((HI, HI), (HI, LO), (LO, HI)):
                            ins = mm(bank(k, D + 2), es[p][:, jt % RE, k * P:(k + 1) * P], H[q][:, jt, :],
                                     start=(jt == 0 and (p, q) == (HI, HI)), stop=(jt == T - 1 and p == LO))
                    ins.then_inc(e_used, 1)

            def block1(b):
                aggregate(0, b, 0)
                aggregate(0, b, 1)
                attend(b, range(0, 2))
                for k in range(TB):
                    if k == 0:
                        pe.wait_ge(agg_lo, (b + 1) * KD)
                    wait_from(pe, g_ev, b * TB + k - 1)
                    project(bank(6 + k % 2, D + 2), agg, slice(k * P, (k + 1) * P), wgs, D + 2).then_inc(g_mm, 1)
                attend(b, range(2, T))

            pe.wait_ge(H_ready, 2)
            block1(0)
            with pe.Fori(1, B) as b:
                block1(b)
            pe.drain().then_inc(l1_done, 1)

            def out2(b):
                for k in range(TB):
                    if k == 0:
                        pe.wait_ge(agg_lo, (B + b + 1) * KD)
                    pe.wait_ge(relu_ready, TB + (b - 1) * TB + k + 1)
                    project(bank(k, D), agg, slice(k * P, (k + 1) * P), wls, D).then_inc(o2_mm, 1)

            pe.wait_ge(l1_done, 4)
            for f in range(KD):
                aggregate(1, 0, f, diag=True)
            pe.wait_ge(w_ready, 3)
            with pe.Fori(1, B) as b:
                aggregate(1, b, 0, diag=True)
                out2(b - 1)
                aggregate(1, b, 1, diag=True)
            out2(B - 1)
            pe.drain().then_inc(l2_done, 1)

            def hidden1(b):
                pe.wait_ge(agg_lo, (2 * B + b + 1) * KD)
                for o in range(KH):
                    pe.wait_ge(h_f, 2 + b * KH + o - 1)
                    for k in range(KD):
                        for p, q in ((HI, HI), (HI, LO), (LO, HI)):
                            ins = mm(bank(o % 2), W1s[p][:, k, o * P:(o + 1) * P], agg[q][:, k, :],
                                     start=(k == 0 and (p, q) == (HI, HI)), stop=(k == KD - 1 and p == LO))
                    ins.then_inc(h_mm, 1)

            def rows(b, ws, width):
                for k in range(TB):
                    n = b * TB + k
                    pe.wait_ge(r_copied, 2 + n - 1)
                    for o in range(KH):
                        if k == 0:
                            pe.wait_ge(h_lo, 2 + b * KH + o + 1)
                        for p, q in ((HI, HI), (HI, LO), (LO, HI)):
                            ins = mm(bank(2 + k % 2, width), hh[p][:, o, k * P:(k + 1) * P], ws[q][:, o, :],
                                     start=(o == 0 and (p, q) == (HI, HI)), stop=(o == KH - 1 and p == LO))
                    ins.then_inc(r_mm, 1)

            pe.wait_ge(l2_done, 4)
            for f in range(KD):
                aggregate(2, 0, f)
            pe.wait_ge(wp_ready, 2)
            with pe.Fori(1, B) as b:
                aggregate(2, b, 0)
                hidden1(b - 1)
                rows(b - 1, W2s, HID)
                aggregate(2, b, 1)
            hidden1(B - 1)
            rows(B - 1, W2s, HID)
            pe.drain().then_inc(h1_done, 1)

            def hidden2(b, o):
                pe.wait_ge(h_f, 2 + (B + b - 1) * KH + o + 1)
                for jt in range(T):
                    for part in (HI, LO):
                        ins = mm(bank(4 + o), g16(jt, part, o * P, P), adjT[:, jt, bass.ds(b * CB, CB)],
                                 start=(jt == 0 and part == HI), stop=(jt == T - 1 and part == LO))
                ins.then_inc(h_mm, 1)

            for jt in range(T):
                pe.wait_ge(c3_lo, jt + 1)
                for o in range(KH):
                    for part in (HI, LO):
                        ins = mm(bank(4 + o), g16(jt, part, o * P, P), adjT[:, jt, 0:CB],
                                 start=(jt == 0 and part == HI), stop=(jt == T - 1 and part == LO))
                    if jt == T - 1:
                        ins.then_inc(h_mm, 1)
            pe.wait_ge(wp_ready, 3)
            with pe.Fori(1, B) as b:
                hidden2(b, 0)
                rows(B + b - 1, W3s, D)
                for o in range(1, KH):
                    hidden2(b, o)
            rows(2 * B - 1, W3s, D)
            pe.drain().then_inc(h2_done, 1)

            def out3(t, u):
                wait_from(pe, o3_read, t - 1)
                for jt in range(T):
                    if isinstance(t, int) and t == 0:
                        pe.wait_ge(c3_lo, T + jt + 1)
                    ins = mm(bank(u), adjT[:, jt, bass.ds(t * P, P)], f16[:, jt, :], start=(jt == 0),
                             stop=(jt == T - 1))
                ins.then_inc(o3_mm, 1)

            out3(0, 0)
            out3(1, 1)
            with pe.Fori(1, T // 2) as i:
                for u in range(2):
                    out3(2 * i + u, u)

        @block.scalar
        def _(act):
            own = Chain(act, act_own)
            for s, n in CREDITS["act"]:
                act.sem_inc(s, n)
            run = nc.scalar.activation

            for n in range(P0_GROUPS):
                act.wait_ge(p0_mm, n + 1)
                b, f, t = n // KD % B, n % KD, n - 4 * B
                to = (xT0[HI][:, f, b * CB:(b + 1) * CB] if n < 2 * B else
                      hT[HI][:, f, b * CB:(b + 1) * CB] if n < 4 * B else sup[:, t, 0:D])
                run(to, bank(4 + n % 4, CB if n < 4 * B else D), ACT.Copy).then_inc(p0_hi, 1)

            def cast(t):
                for k in range(2):
                    act.wait_ge(adj_landed[k], 16 * (t + 1))
                    wait_from(act, adj_tr, 2 * (t - 1) + k + 1)
                    wait_from(act, fill_ready, t)
                    run(adjb[:, k * HALF:(k + 1) * HALF], adjf[:, k, :], ACT.Copy,
                        accum_out=tile(deg, t)[:, k:k + 1]).then_inc(adj_cast, 1)

            def pt_high(t, g):
                act.wait_ge(pt_tr, t * TB + g + 1)
                run(PT[HI][:, 4 * g:4 * g + 4, :], bank(4 + g % 2).rearrange("p (a b) -> p a b", b=P), ACT.Copy) \
                    .then_inc(pt_hi, 1)

            def round0(t, u, more=True):
                if not (isinstance(t, int) and t == 0):
                    for g in range(4):
                        pt_high(t - 1, g)
                act.wait_ge(e_maxed, t + 1)
                wait_from(act, pv_read, t - 1)
                run(em[:, u, :], em[:, u, :], ACT.Exp, bias=negm[:, u:u + 1], accum_out=Z[:, u:u + 1]) \
                    .then_inc(exp_done, 1)
                act.wait_ge(adj_tr, 2 * t + 2)
                run(adjT[:, T // 2:T, bass.ds(t * P, P)],
                    ps[:, 6, :].bitcast(BF16).rearrange("p (a b) -> p a b", b=P), ACT.Copy).then_inc(adj_ev[1], 1)
                if more:
                    cast(t + 1)

            cast(0)
            act.wait_ge(node_neg, 1)
            run(nl[:, :], nl[:, :], ACT.Exp, bias=nst[:, 2:3], accum_out=nst[:, 3:4]).then_inc(node_exp, 1)
            round0(0, 0)
            round0(1, 1)
            with act.Fori(1, T // 2 - 1) as i:
                for u in range(2):
                    round0(2 * i + u, u)
            round0(T - 2, 0)
            round0(T - 1, 1, more=False)
            for g in range(4):
                pt_high(T - 1, g)
            act.drain().then_inc(l0_done, 1)

            act.wait_ge(l0_done, 4)
            for n in range(P1_GROUPS):
                act.wait_ge(p1_mm, n + 1)
                b, f, t = n // KD, n % KD, n - 2 * B
                if n < 2 * B:
                    run(xT1[HI][:, f, b * CB:(b + 1) * CB], bank(n % 4), ACT.Copy).then_inc(p1_hi, 1)
                elif n < P1_SPLITS:
                    own.link(run(vj[:, t, :], ps[:, n % 4, D:D + 1], ACT.Exp, scale=-SLOPE))
                    run(H[HI][:, t, 0:D], bank(n % 4, D), ACT.Copy, scale=vj[:, t, :]).then_inc(p1_hi, 1)
                else:
                    b = n - P1_SPLITS
                    run(slrow[:, b * CB:(b + 1) * CB], bank(n % 4), ACT.Copy).then_inc(p1_hi, 1)
            run(H[HI][:, :, D:D + 1], vj[:, :, :], ACT.Copy).then_inc(H_ready, 1)
            act.wait_ge(ex_ready, 1)
            run(wi[:, :], ex[:, :, 1], ACT.Exp, scale=SLOPE).then_inc(w_exp, 1)

            def agg_high(layer, b, f):
                act.wait_ge(agg_mm, (layer * B + b) * KD + f + 1)
                run(agg[HI][:, f, :], bank(4 + f), ACT.Copy, scale=1.0 / XS).then_inc(agg_hi, 1)

            def edge_exp(b, jt):
                n = b * T + jt
                act.wait_ge(tm_ready, n + 1)
                wait_from(act, es_lo, n + 1 - RE)
                run(ef[:, jt % RE, :], tm[:, jt % 2, :], ACT.Exp, scale=SLOPE - 1.0).then_inc(ef_ready, 1)

            def block1(b):
                for jt in range(RE):
                    edge_exp(b, jt)
                wait_from(act, g_mm, b * TB)
                for f in range(KD):
                    agg_high(0, b, f)
                for jt in range(RE, T - 4):
                    edge_exp(b, jt)
                act.wait_ge(g_ev, (b + 1) * TB)
                run(gate[:, :, :], gate[:, :, :], ACT.Tanh, scale=0.5).then_inc(gate_tanh, 1)
                for jt in range(T - 4, T):
                    edge_exp(b, jt)
                act.wait_ge(gate_ready, b + 1)
                for k0 in range(0, TB, 2):
                    for k in (k0, k0 + 1):
                        wait_from(act, z_ready, b * TB + k - 1)
                        run(z1[:, k % 2, :], g4[:, k, :], ACT.Copy, scale=gate[:, k, 1:2]).then_inc(z1_ready, 1)
                    for k in (k0, k0 + 1):
                        act.wait_ge(z_ready, b * TB + k + 1)
                        own.link(run(y[:, k % 2, :], y[:, k % 2, :], ACT.Tanh, scale=0.5))
                        run(y[:, k % 2, :], y[:, k % 2, :], ACT.Copy, scale=0.5, bias=0.5).then_inc(sig_ready, 1)

            block1(0)
            with act.Fori(1, B) as b:
                own.enter(b - 1, TB)
                block1(b)
            own.leave(B - 1)
            act.drain().then_inc(l1_done, 1)

            act.wait_ge(l1_done, 4)
            act.wait_ge(dsc_ready, 1)
            for t in range(T):
                run(x16[:, HI, t, :], x[:, t, :], ACT.Copy, scale=dsc[:, t:t + 1]).then_inc(conv_hi, 1)

            def relu2(b):
                for k in range(TB):
                    n = b * TB + k
                    act.wait_ge(o2_mm, n + 1)
                    act.wait_ge(y2_ready, 2 + n - 1)
                    run(xb[:, k % 2, :], bank(k, D), ACT.Relu, scale=dinv[:, bass.ds(n, 1)]).then_inc(relu_ready, 1)

            agg_high(1, 0, 0)
            with act.Fori(1, B) as b:
                agg_high(1, b - 1, 1)
                relu2(b - 1)
                agg_high(1, b, 0)
            agg_high(1, B - 1, 1)
            relu2(B - 1)
            act.drain().then_inc(l2_done, 1)

            act.wait_ge(l2_done, 4)
            for t in range(T):
                run(x16[:, HI, t, :], x[:, t, :], ACT.Copy, scale=XS).then_inc(conv_hi, 1)
            act.wait_ge(wh_landed, 80)

            def hidden(b, o, frm, bias, scale):
                n = b * KH + o
                act.wait_ge(h_mm, n + 1)
                act.wait_ge(h_lo, 2 + n - 1)
                run(hf[:, o % 2, :], bank(frm), ACT.Relu, bias=bias[:, o:o + 1], scale=scale).then_inc(h_f, 1)

            def rows(b, to, first, width):
                for k in range(TB):
                    act.wait_ge(r_mm, b * TB + k + 1)
                    run(tile(to, b * TB + k + first), bank(2 + k % 2, width), ACT.Copy).then_inc(r_copied, 1)

            def mid(b):
                for o in range(KH):
                    hidden(b, o, o % 2, b1c, 1.0)
                rows(b, G, AHEAD, HID)

            agg_high(2, 0, 0)
            with act.Fori(1, B) as b:
                agg_high(2, b - 1, 1)
                mid(b - 1)
                agg_high(2, b, 0)
            agg_high(2, B - 1, 1)
            mid(B - 1)
            act.drain().then_inc(h1_done, 1)

            act.wait_ge(scale_ready, 1)
            for t in range(T):
                wait_from(act, c3_lo, t - AHEAD + 1)
                run(g16(t, HI), G[:, t + AHEAD, :], ACT.Copy, scale=g1[:, 2:3]).then_inc(c3_hi, 1)
            act.wait_ge(h1_done, 4)
            for o in range(KH):
                hidden(B, o, 4 + o, b2c, g1[:, 3:4])
            with act.Fori(1, B) as b:
                rows(B + b - 1, F, -B * TB, D)
                for o in range(KH):
                    hidden(B + b, o, 4 + o, b2c, g1[:, 3:4])
            rows(2 * B - 1, F, -B * TB, D)
            act.drain().then_inc(h2_done, 1)

            act.wait_ge(scale_ready, 2)
            for t in range(T):
                run(f16[:, t, 0:D], F[:, t, :], ACT.Copy, scale=g1[:, 2:3]).then_inc(c3_hi, 1)

        @block.vector
        def _(dve):
            own = Chain(dve, dve_own)
            for s, n in CREDITS["dve"]:
                dve.sem_inc(s, n)
            tt, stt, ts = nc.vector.tensor_tensor, nc.vector.scalar_tensor_tensor, nc.vector.tensor_scalar

            def split(full, parts):
                own.link(nc.vector.tensor_copy(parts[HI][:, :, :], full))
                own.link(tt(parts[LO][:, :, :], full, parts[HI][:, :, :].bitcast(F32), ALU.subtract))

            def low(to, frm, high):
                return tt(to, frm, high.bitcast(F32), ALU.subtract)

            def normed(m, u, to):
                dve.wait_ge(rstd_ready, m + 1)
                ts(to, y[:, u, :], mv[:, u, 0:1], rstd[:, u, 1:2], ALU.subtract, ALU.mult).then_inc(y_normed, 1)

            def y_free(m):
                dve.wait_ge(y_normed, m - 1)

            def moments(u):
                own.link(nc.vector.bn_stats(stats[:, u, :], y[:, u, :]))
                pause(dve, turns)
                nc.vector.bn_aggr(mv[:, u, :], stats[:, u, :]).then_inc(var_ready, 1)

            dve.wait_ge(w0_landed, 64)
            dve.wait_ge(const_ready, 3)
            split(we[:, :, :], wes)
            own.link(nc.vector.tensor_copy(w0s[HI][:, :, :], w0x[:, :, :]))
            low(w0s[LO][:, :, :], w0x[:, :, :], w0s[HI][:, :, :]).then_inc(w_ready, 1)
            for n in range(P0_GROUPS):
                dve.wait_ge(p0_hi, n + 1)
                b, f, t = n // KD % B, n % KD, n - 4 * B
                if n < 4 * B:
                    s = xT0 if n < 2 * B else hT
                    cols = slice(b * CB, (b + 1) * CB)
                    low(s[LO][:, f, cols], bank(4 + n % 4), s[HI][:, f, cols]).then_inc(p0_lo, 1)
                else:
                    own.link(nc.vector.tensor_copy(nl[:, t:t + 1], ps[:, 4 + n % 4, D:D + 1]))
                    low(sup[:, t, D:2 * D], bank(4 + n % 4, D), sup[:, t, 0:D]).then_inc(p0_lo, 1)
            nc.vector.reduce_max(nst[:, 0:1], nl[:, :], AX_X).then_inc(node_max, 1)
            dve.wait_ge(node_gmax, 1)
            ts(nst[:, 2:3], nst[:, 1:2], -1.0, None, ALU.mult).then_inc(node_neg, 1)

            def masked_max(t, u, h):
                dve.wait_ge(e_mm, 2 * t + h + 1)
                wait_from(dve, pv_mm, t - 1)
                pause(dve, turns)
                banks = ps[:, 2 * h:2 * h + 2, :].rearrange("p a b -> p (a b)")
                cols = slice(h * HALF, (h + 1) * HALF)
                nc.vector.tensor_tensor_reduce(out=em[:, u, cols], in0=banks, in1=fill[:, cols], scale=1.0,
                                               scalar=-3.0e38, op0=ALU.add, op1=ALU.max,
                                               accum_out=mx[:, u, h:h + 1]).then_inc(e_read, 1)

            def pt_low(t, g):
                dve.wait_ge(pt_hi, t * TB + g + 1)
                c = slice(4 * g, 4 * g + 4)
                low(PT[LO][:, c, :], bank(4 + g % 2).rearrange("p (a b) -> p a b", b=P), PT[HI][:, c, :]) \
                    .then_inc(pt_lo, 1)

            def final0(t, u):
                dve.wait_ge(exp_done, t + 1)
                own.link(ts(rowf[:, u, 0:1], negm[:, u:u + 1], BIG / 2, nl[:, bass.ds(t, 1)], ALU.is_lt, ALU.mult))
                own.link(nc.vector.reciprocal(rowf[:, u, 1:2], Z[:, u:u + 1]))
                own.link(tt(rowf[:, u, 2:3], rowf[:, u, 0:1], rowf[:, u, 1:2], ALU.mult))
                dve.wait_ge(pv_mm, t + 1)
                dve.wait_ge(xb_ready, t + 1)
                stt(y[:, u, :], bank(7, D), rowf[:, u, 2:3], xb[:, u, :], ALU.mult, ALU.add).then_inc(xb_used, 1)
                dve.wait_ge(xb_used, t + 1)
                stt(y[:, u, :], ps[:, 7, D:2 * D], rowf[:, u, 2:3], y[:, u, :], ALU.mult, ALU.add) \
                    .then_inc(pv_read, 1)
                dve.wait_ge(pv_read, t + 1)
                moments(u)

            def round0(t, u):
                first = isinstance(t, int) and t == 0
                if not (isinstance(t, int) and t < 2):
                    normed(t - 2, u, tile(x, t - 2))
                dve.wait_ge(adj_cast, 2 * t + 2)
                ts(fill[:, :], adjb[:, :], -1.0, BIG, ALU.add, ALU.mult).then_inc(fill_ready, 1)
                dve.wait_ge(fill_ready, t + 1)
                masked_max(t, u, 0)
                if not first:
                    pt_low(t - 1, 0)
                    pt_low(t - 1, 1)
                masked_max(t, u, 1)
                dve.wait_ge(e_read, 2 * t + 2)
                ts(negm[:, u:u + 1], mx[:, u, 0:1], mx[:, u, 1:2], -1.0, ALU.max, ALU.mult).then_inc(e_maxed, 1)
                dve.wait_ge(adj_tr, 2 * t + 1)
                nc.vector.tensor_copy(adjT[:, 0:T // 2, bass.ds(t * P, P)],
                                      ps[:, 6, :].bitcast(BF16).rearrange("p (a b) -> p a b", b=P)) \
                    .then_inc(adj_ev[0], 1)
                if not first:
                    pt_low(t - 1, 2)
                    pt_low(t - 1, 3)
                    final0(t - 1, 1 - u)

            LINKS0 = 4
            round0(0, 0)
            dve.wait_ge(node_sum, 1)
            own.link(nc.vector.reciprocal(nst[:, 3:4], nst[:, 4:5]))
            own.link(ts(nl[:, :], nl[:, :], nst[:, 3:4], None, ALU.mult))
            round0(1, 1)
            with dve.Fori(0, T // 2 - 1) as i:
                own.enter(i, 2 * LINKS0)
                for u in range(2):
                    round0(2 * i + 2 + u, u)
            own.leave(T // 2 - 1)
            normed(T - 2, 0, x[:, T - 2, :])
            for g in range(4):
                pt_low(T - 1, g)
            final0(T - 1, 1)
            normed(T - 1, 1, x[:, T - 1, :])
            dve.drain().then_inc(l0_done, 1)

            dve.wait_ge(l0_done, 4)
            for n in range(2 * B):
                b, f = n // KD, n % KD
                cols = slice(b * CB, (b + 1) * CB)
                dve.wait_ge(p1_hi, n + 1)
                low(xT1[LO][:, f, cols], bank(n % 4), xT1[HI][:, f, cols]).then_inc(p1_lo, 1)
            dve.wait_ge(wt1_landed, 160)
            for k in range(KD):
                for g, c in ((0, D), (1, 0)):
                    own.link(nc.vector.tensor_tensor_reduce(
                        out=scr[:, :], in0=wsx[:, k, 0:D], in1=arow[:, c:c + D], scale=1.0, scalar=0.0,
                        op0=ALU.mult, op1=ALU.add, accum_out=wsx[:, k, D + g:D + g + 1]))
            split(wgx[:, :, :], wgs)
            own.link(nc.vector.tensor_copy(wss[HI][:, :, :], wsx[:, :, :]))
            low(wss[LO][:, :, :], wsx[:, :, :], wss[HI][:, :, :]).then_inc(w_ready, 1)
            for n in range(2 * B, P1_SPLITS):
                t = n - 2 * B
                dve.wait_ge(p1_hi, n + 1)
                own.link(nc.vector.tensor_copy(ex[:, t, :], ps[:, n % 4, D:D + 4]))
                stt(H[LO][:, t, 0:D], bank(n % 4, D), vj[:, t, :], H[HI][:, t, 0:D].bitcast(F32),
                    ALU.mult, ALU.subtract).then_inc(p1_lo, 1)
                dve.wait_ge(conv_hi, t + 1)
                stt(x16[:, LO, t, :], x[:, t, :], XS, x16[:, HI, t, :], ALU.mult, ALU.subtract) \
                    .then_inc(conv_lo, 1)
            own.link(tt(ex[:, :, 2:4], ex[:, :, 2:4], bab[:, :, :].to_broadcast([P, T, 2]), ALU.add))
            dve.sem_inc(ex_ready, 1)
            for part in (HI, LO):
                own.link(nc.vector.memset(H[part][:, :, D + 1:D + 2].bitcast(F32), 0.0))
            dve.wait_ge(H_ready, 1)
            low(H[LO][:, :, D:D + 1], vj[:, :, :], H[HI][:, :, D:D + 1]).then_inc(H_ready, 1)
            dve.wait_ge(dinv_ready, 1)
            ts(dsc[:, :], dinv[:, :], XS, None, ALU.mult).then_inc(dsc_ready, 1)
            dve.wait_ge(w_exp, 1)
            own.link(ts(wi[:, :], wi[:, :], EPS, None, ALU.mult))
            dve.wait_ge(p1_mm, P1_GROUPS)
            dve.wait_ge(p1_hi, P1_GROUPS)

            def agg_low(layer, b, f):
                dve.wait_ge(agg_hi, (layer * B + b) * KD + f + 1)
                stt(agg[LO][:, f, :], bank(4 + f), 1.0 / XS, agg[HI][:, f, :].bitcast(F32),
                    ALU.mult, ALU.subtract).then_inc(agg_lo, 1)

            def edge_scores(b, jt):
                n = b * T + jt
                own.link(ts(nb[:, jt % 2, :], adjT[:, jt, bass.ds(b * CB, CB)], -1.0, -FAR, ALU.add, ALU.mult))
                wait_from(dve, ef_ready, n - 1)
                stt(tm[:, jt % 2, :], slrow[:, bass.ds(b * CB, CB)], ex[:, jt, 0:1], nb[:, jt % 2, :],
                    ALU.add, ALU.max).then_inc(tm_ready, 1)

            def edge_low(b, jt):
                n = b * T + jt
                dve.wait_ge(es_hi, n + 1)
                wait_from(dve, e_used, n + 1 - RE)
                low(es[LO][:, jt % RE, :], ef[:, jt % RE, :], es[HI][:, jt % RE, :]).then_inc(es_lo, 1)

            def neighbours(b, k):
                n = b * TB + k
                dve.wait_ge(g_mm, n + 1)
                own.link(tt(g4[:, k, :], bank(6 + k % 2, D), brow[:, :], ALU.add))
                tt(gate[:, k, :], ps[:, 6 + k % 2, D:D + 2], tile(ex, n)[:, 2:4], ALU.add).then_inc(g_ev, 1)

            def final1(b, k):
                n = b * TB + k
                y_free(T + n)
                dve.wait_ge(z1_ready, n + 1)
                stt(y[:, k % 2, :], bank(k, D), rz[:, k:k + 1], z1[:, k % 2, :], ALU.mult, ALU.add) \
                    .then_inc(z_ready, 1)

            def residual1(b, k):
                n = b * TB + k
                dve.wait_ge(sig_ready, n + 1)
                own.link(tt(y[:, k % 2, :], y[:, k % 2, :], tile(x, n), ALU.add))
                moments(k % 2)

            LINKS1 = T + TB + 3 + 2 * TB

            def block1(b):
                for jt in range(3):
                    edge_scores(b, jt)
                edge_low(b, 0)
                edge_scores(b, 3)
                for jt in range(1, 4):
                    edge_low(b, jt)
                for f in range(KD):
                    agg_low(0, b, f)
                edge_scores(b, 4)
                edge_scores(b, 5)
                edge_low(b, 4)
                edge_scores(b, 6)
                edge_low(b, 5)
                edge_scores(b, 7)
                for k in range(TB):
                    neighbours(b, k)
                for jt in range(6, T):
                    edge_low(b, jt)
                    if jt + 2 < T:
                        edge_scores(b, jt + 2)
                    if jt == T - 3:
                        dve.wait_ge(gate_tanh, b + 1)
                        ts(gate[:, :, :], gate[:, :, :], 0.5, 0.5, ALU.mult, ALU.add).then_inc(gate_ready, 1)
                dve.wait_ge(e_used, (b + 1) * T)
                own.link(tt(rz[:, :], ps[:, 0:TB, D:D + 1].rearrange("p a b -> p (a b)"),
                            wi[:, bass.ds(b * TB, TB)], ALU.add))
                own.link(nc.vector.reciprocal(rz[:, :], rz[:, :]))
                dve.wait_ge(gate_ready, b + 1)
                own.link(tt(rz[:, :], rz[:, :], gate[:, :, 0], ALU.mult))
                for k0 in range(0, TB, 2):
                    final1(b, k0)
                    final1(b, k0 + 1)
                    residual1(b, k0)
                    residual1(b, k0 + 1)
                    for k in (k0, k0 + 1):
                        normed(T + b * TB + k, k % 2, tile(x, b * TB + k))

            block1(0)
            with dve.Fori(1, B) as b:
                own.enter(b - 1, LINKS1)
                block1(b)
            own.leave(B - 1)
            dve.drain().then_inc(l1_done, 1)

            dve.wait_ge(l1_done, 4)
            for t in range(T):
                dve.wait_ge(conv_hi, T + t + 1)
                stt(x16[:, LO, t, :], x[:, t, :], dsc[:, t:t + 1], x16[:, HI, t, :], ALU.mult, ALU.subtract) \
                    .then_inc(conv_lo, 1)
            dve.wait_ge(wt2_landed, 16)
            own.link(nc.vector.tensor_copy(wls[HI][:, :, :], wlf[:, :, :]))
            low(wls[LO][:, :, :], wlf[:, :, :], wls[HI][:, :, :]).then_inc(w_ready, 1)

            def block2(b):
                for k in range(TB):
                    n = b * TB + k
                    dve.wait_ge(relu_ready, TB + n + 1)
                    if k >= 2:
                        normed(2 * T + n - 2, k % 2, tile(x, n - 2))
                    y_free(2 * T + n)
                    tt(y[:, k % 2, :], xb[:, k % 2, :], tile(x, n), ALU.add).then_inc(y2_ready, 1)
                    dve.wait_ge(y2_ready, 2 + n + 1)
                    moments(k % 2)
                for k in (TB - 2, TB - 1):
                    normed(2 * T + b * TB + k, k % 2, tile(x, b * TB + k))

            agg_low(1, 0, 0)
            with dve.Fori(1, B) as b:
                own.enter(b - 1, TB)
                agg_low(1, b - 1, 1)
                block2(b - 1)
                agg_low(1, b, 0)
            own.leave(B - 1)
            agg_low(1, B - 1, 1)
            block2(B - 1)
            dve.drain().then_inc(l2_done, 1)

            dve.wait_ge(l2_done, 4)
            for t in range(T):
                dve.wait_ge(conv_hi, 2 * T + t + 1)
                stt(x16[:, LO, t, :], x[:, t, :], XS, x16[:, HI, t, :], ALU.mult, ALU.subtract) \
                    .then_inc(conv_lo, 1)

            def hidden_low(b):
                for o in range(KH):
                    dve.wait_ge(h_hi, b * KH + o + 1)
                    low(hh[LO][:, o, :], hf[:, o % 2, :], hh[HI][:, o, :]).then_inc(h_lo, 1)

            def rows_max(b, of, ahead, first=0):
                for k in range(TB):
                    n = b * TB + k
                    dve.wait_ge(r_copied, 2 + n + 1)
                    nc.vector.tensor_reduce(gm[:, bass.ds(n - first, 1)], tile(of, n - first + ahead), AX_X,
                                            ALU.max, apply_absolute_value=True).then_inc(r_maxed, 1)

            def scales(n):
                nc.vector.reduce_max(g1[:, 0:1], gm[:, :], AX_X).then_inc(tmax_ready, 1)
                dve.wait_ge(gmax_ready, n)
                own.link(ts(g1[:, 3:4], g1[:, 1:2], 1e-30, 1.0 / TOP, ALU.max, ALU.mult))
                nc.vector.reciprocal(g1[:, 2:3], g1[:, 3:4]).then_inc(scale_ready, 1)

            agg_low(2, 0, 0)
            with dve.Fori(1, B) as b:
                agg_low(2, b - 1, 1)
                hidden_low(b - 1)
                rows_max(b - 1, G, AHEAD)
                agg_low(2, b, 0)
            agg_low(2, B - 1, 1)
            hidden_low(B - 1)
            rows_max(B - 1, G, AHEAD)
            dve.wait_ge(r_maxed, T)
            dve.drain().then_inc(h1_done, 1)
            scales(1)
            for t in range(T):
                dve.wait_ge(c3_hi, t + 1)
                stt(g16(t, LO), G[:, t + AHEAD, :], g1[:, 2:3], g16(t, HI), ALU.mult, ALU.subtract) \
                    .then_inc(c3_lo, 1)
            hidden_low(B)
            with dve.Fori(1, B) as b:
                rows_max(B + b - 1, F, 0, T)
                hidden_low(B + b)
            rows_max(2 * B - 1, F, 0, T)
            dve.wait_ge(r_maxed, 2 * T)
            dve.drain().then_inc(h2_done, 1)
            scales(2)
            for t in range(T):
                dve.wait_ge(c3_hi, T + t + 1)
                stt(f16[:, t, D:2 * D], F[:, t, :], g1[:, 2:3], f16[:, t, 0:D], ALU.mult, ALU.subtract) \
                    .then_inc(c3_lo, 1)

            def final3(t, u):
                y_free(3 * T + t)
                dve.wait_ge(o3_mm, t + 1)
                dve.wait_ge(xb_ready, T + t + 1)
                stt(y[:, u, :], bank(u, D), g1[:, 3:4], xb[:, u, :], ALU.mult, ALU.add).then_inc(xb_used, 1)
                dve.wait_ge(xb_used, T + t + 1)
                stt(y[:, u, :], ps[:, u, D:2 * D], g1[:, 3:4], y[:, u, :], ALU.mult, ALU.add).then_inc(o3_read, 1)
                dve.wait_ge(o3_read, t + 1)
                moments(u)

            def store3(t, u, stored):
                wait_from(dve, o_stored[u], 16 * stored)
                normed(3 * T + t, u, ob[:, u, :])

            final3(0, 0)
            final3(1, 1)
            store3(0, 0, 0)

            def pair3(i):
                final3(2 * i, 0)
                store3(2 * i - 1, 1, i - 1)
                final3(2 * i + 1, 1)
                store3(2 * i, 0, i)

            pair3(1)
            with dve.Fori(2, T // 2) as i:
                own.enter(i - 2, 2)
                pair3(i)
            own.leave(T // 2 - 2)
            store3(T - 1, 1, T // 2 - 1)
    return nc


_INS = ['x', 'adj', 'L0_gnn_weight', 'L0_gnn_bias', 'L0_gnn_node_w', 'L0_gnn_edge_w', 'L1_gnn_W_sa', 'L1_gnn_a_sa',
        'L1_gnn_W_gcnb', 'L1_gnn_b_gcnb', 'L1_gnn_Wa', 'L1_gnn_ba', 'L1_gnn_Wb', 'L1_gnn_bb', 'L2_gnn_weight',
        'L3_gnn_W1', 'L3_gnn_b1', 'L3_gnn_W2', 'L3_gnn_b2', 'L3_gnn_W3', 'L3_gnn_b3']


def kernel(**inputs):
    import concourse.bacc as bacc
    from concourse.bass_utils import run_bass_kernel_spmd

    nc = bacc.Bacc("TRN2", target_bir_lowering=False, num_devices=1)
    arrays, args = {}, []
    for name in _INS:
        a = np.ascontiguousarray(inputs[name])
        arrays[f"in_{name}"] = a
        args.append(nc.dram_tensor(f"in_{name}", a.shape, mybir.dt.from_np(a.dtype), kind="ExternalInput").ap())
    out = nc.dram_tensor("out", inputs["x"].shape, F32, kind="ExternalOutput").ap()
    build(nc, *args, out)
    return run_bass_kernel_spmd(nc, [arrays], core_ids=[0]).results[0]["out"]
```

```python
from contextlib import ExitStack

import numpy as np
import concourse.bass as bass
from concourse import mybir

F32 = mybir.dt.float32
F32R = mybir.dt.float32r
BF16 = mybir.dt.bfloat16
F16 = mybir.dt.float16
ALU = mybir.AluOpType
ACT = mybir.ActivationFunctionType
AX_X = mybir.AxisListType.X
RMAX = bass.bass_isa.ReduceOp.max
RADD = bass.bass_isa.ReduceOp.add
HI, LO = 0, 1


class Chain:

    def __init__(self, eng, sem):
        self.eng, self.sem, self.base, self.n = eng, sem, 0, 0

    def link(self, ins):
        ins.then_inc(self.sem, 1)
        self.n += 1
        self.eng.wait_ge(self.sem, self.base + self.n)

    def enter(self, i, per_round):
        self.start, self.per_round = self.base + self.n, per_round
        self.base, self.n = i * per_round + self.start, 0

    def leave(self, rounds):
        assert self.n == self.per_round, (self.n, self.per_round)
        self.base, self.n = self.start + rounds * self.per_round, 0


def wait_from(eng, sem, value):
    if not isinstance(value, int) or value > 0:
        eng.wait_ge(sem, value)


def pause(eng, turns):
    eng.sem_inc(turns, 1)


def tile(tensor, t):
    return tensor[:, bass.ds(t, 1), :].rearrange("p a d -> p (a d)")


def build(nc, x_in, adj_in, w0_in, b0_in, node_in, edge_in, wsa_in, asa_in, wg_in, bg_in,
          wa_in, ba_in, wb_in, bb_in, wl2_in, W1_in, b1_in, W2_in, b2_in, W3_in, b3_in, out):
    N, D = x_in.shape
    HID = W1_in.shape[1]
    P = 128
    T = N // P
    KD = D // P
    KH = HID // P
    CB = 512
    B = N // CB
    TB = CB // P
    HALF = N // 2
    BIG = 9.0e15
    FAR = 1.0e38
    EPS = 1e-5
    SLOPE = 0.01
    XS = 2048.0
    TOP = 16384.0
    RE = 4
    PAIRS = T // 2
    G_BANK = (6, 7, 4, 5)
    AGG_TILES = (4, 3, 3, 2, 2, 2)
    AHEAD = 3
    P0_GROUPS = 2 * KD * B + T
    P1_SPLITS = KD * B + T
    P1_GROUPS = P1_SPLITS + B
    assert HID == CB and N == 2 * 8 * P

    def w_tiles(w):
        return w.rearrange("(k p) n -> p k n", p=P)

    def vec_row(v):
        return v.rearrange("(a n) -> a n", a=1).to_broadcast([P, v.shape[0]])

    ctx = ExitStack()
    with ctx:
        def sb(stack, name, shape, dt=F32):
            return stack.enter_context(nc.sbuf_tensor(name, shape, dt))

        def pair(stack, name, shape, dt=F32R):
            return [sb(stack, name + n, shape, dt) for n in ("_hi", "_lo")]

        def sem(name):
            return ctx.enter_context(nc.semaphore(name))

        adjT = sb(ctx, "adjT", [P, T, N], BF16)
        x = sb(ctx, "x", [P, T, D])
        ident = sb(ctx, "ident", [P, P])
        identb = sb(ctx, "identb", [P, P], BF16)
        deg = sb(ctx, "deg", [P, T, 2])
        dinv = sb(ctx, "dinv", [P, T])
        dsc = sb(ctx, "dsc", [P, T])
        ones = sb(ctx, "ones", [P, T])
        epsc = sb(ctx, "epsc", [P, 1])
        mhalf = sb(ctx, "mhalf", [P, T])
        stats = sb(ctx, "stats", [P, 2, 6])
        mv = sb(ctx, "mv", [P, 2, 2])
        rstd = sb(ctx, "rstd", [P, 2, 2])
        y = sb(ctx, "y", [P, 2, D])
        xb = sb(ctx, "xb", [P, 2, D])
        brow = sb(ctx, "brow", [P, D])
        gm = sb(ctx, "gm", [P, T])
        g1 = sb(ctx, "g1", [P, 4])

        adjf = sb(ctx, "adjf", [P, 2, HALF])
        room = adjf[:, :, :].rearrange("p a b -> p (a b)")

        def in_room(first, *shape):
            flat = room[:, first:first + int(np.prod(shape))]
            return flat.rearrange("p (a b) -> p a b", a=shape[0]) if len(shape) == 2 else flat

        wsx = in_room(0, KD, D + 4)
        wgx = in_room(KD * (D + 4), KD, D + 2)
        arow = in_room(KD * (2 * D + 6), 2 * D)
        scr = in_room(KD * (2 * D + 6) + 2 * D, D)
        wlf = in_room(0, KD, D)
        W2f = in_room(0, KH, HID)
        W3f = in_room(0, KH, D)
        ob = in_room(KH * D, 2, D)

        lay0 = ExitStack()
        hT = pair(lay0, "hT", [P, KD, N])
        sup = sb(lay0, "sup", [P, T, 2 * D], F32R)
        nl = sb(lay0, "nl", [P, T])
        nst = sb(lay0, "nst", [P, 5])
        hst = pair(lay0, "hst", [P, 2, KD, P])
        pre0 = ExitStack()
        w0x = sb(pre0, "w0x", [P, KD, D + 2])
        we = sb(pre0, "we", [P, KD, D])
        w0s = pair(pre0, "w0s", [P, KD, D + 2])
        wes = pair(pre0, "wes", [P, KD, D])
        xT0 = pair(pre0, "xT0", [P, KD, N])
        pre0.close()
        main0 = ExitStack()
        em = sb(main0, "em", [P, 2, N])
        PT = pair(main0, "PT", [P, T, P])
        adjb = sb(main0, "adjb", [P, N], BF16)
        fill = sb(main0, "fill", [P, N], BF16)
        mx = sb(main0, "mx", [P, 2, 2])
        negm = sb(main0, "negm", [P, 2])
        Z = sb(main0, "Z", [P, 2])
        rowf = sb(main0, "rowf", [P, 2, 3])
        main0.close()
        lay0.close()

        lay123 = ExitStack()
        x16 = sb(lay123, "x16", [P, 2, T, D], F16)
        agg = pair(lay123, "agg", [P, KD, CB])
        lay1 = ExitStack()
        H = pair(lay1, "H", [P, T, D + 2])
        slrow = sb(lay1, "slrow", [P, N])
        ex = sb(lay1, "ex", [P, T, 4])
        vj = sb(lay1, "vj", [P, T, 1])
        wi = sb(lay1, "wi", [P, T])
        bab = sb(lay1, "bab", [P, 1, 2])
        wgs = pair(lay1, "wgs", [P, KD, D + 2])
        pre1 = ExitStack()
        wss = pair(pre1, "wss", [P, KD, D + 4])
        wlb = pair(pre1, "wlb", [P, KD, P])
        xT1 = pair(pre1, "xT1", [P, KD, N])
        pre1.close()
        main1 = ExitStack()
        nb = sb(main1, "nb", [P, 2, CB], BF16)
        tm = sb(main1, "tm", [P, RE, CB])
        ef = sb(main1, "ef", [P, RE, CB])
        es = pair(main1, "es", [P, RE, CB])
        g4 = sb(main1, "g4", [P, TB, D])
        gate = sb(main1, "gate", [P, TB, 2])
        rz = sb(main1, "rz", [P, TB])
        z = sb(main1, "z", [P, TB, D])
        main1.close()
        lay1.close()
        lay23 = ExitStack()
        hf = sb(lay23, "hf", [P, 2, CB])
        hh = pair(lay23, "hh", [P, KH, CB])
        b1c = sb(lay23, "b1c", [P, KH])
        b2c = sb(lay23, "b2c", [P, KH])
        w12 = ExitStack()
        W1s = pair(w12, "W1s", [P, KD, HID])
        W2s = pair(w12, "W2s", [P, KH, HID])
        W1f = sb(w12, "W1f", [P, KD, HID])
        w12.close()
        w3 = ExitStack()
        W3s = pair(w3, "W3s", [P, KH, D])
        F = sb(w3, "F", [P, T, D])
        w3.close()
        sb(lay23, "gap", [P, (3 * KD + 2 * KH) * HID])
        wl2 = ExitStack()
        wls = pair(wl2, "wls", [P, KD, D])
        wl2.close()
        G = sb(lay23, "G", [P, T + AHEAD, HID])
        lay23.close()
        lay123.close()

        ps = ctx.enter_context(nc.psum_tensor("ps", [P, 8, CB], F32))

        def bank(n, cols=CB):
            return ps[:, n, 0:cols]

        def g16(t, part, c0=0, cols=HID):
            return G[:, t, :].bitcast(F16)[:, part * HID + c0:part * HID + c0 + cols]

        f16 = x16[:, :, :, :].rearrange("p a t d -> p (a t d)").rearrange("p (t c) -> p t c", t=T)

        x_landed = [sem(f"x_landed{c}") for c in range(B)]
        w0_landed, adj_landed = sem("w0_landed"), [sem(f"adj_landed{k}") for k in range(2)]
        bias1_landed = sem("bias1_landed")
        wt1_landed, wt2_landed = sem("wt1_landed"), sem("wt2_landed")
        wh_landed, w3_landed = sem("wh_landed"), sem("w3_landed")
        const_ready = sem("const_ready")
        w_ready = sem("w_ready")
        wp_hi, wp_ready = sem("wp_hi"), sem("wp_ready")
        p0_mm, p0_hi, p0_lo = sem("p0_mm"), sem("p0_hi"), sem("p0_lo")
        node_max, node_gmax, node_neg = sem("node_max"), sem("node_gmax"), sem("node_neg")
        node_exp, node_sum = sem("node_exp"), sem("node_sum")
        h_staged, e_mm, e_read, e_maxed = sem("h_staged"), sem("e_mm"), sem("e_read"), sem("e_maxed")
        adj_cast, adj_tr, adj_ev = sem("adj_cast"), sem("adj_tr"), [sem(f"adj_ev{k}") for k in range(2)]
        fill_ready, exp_done = sem("fill_ready"), sem("exp_done")
        pt_tr, pt_hi, pt_lo = sem("pt_tr"), sem("pt_hi"), sem("pt_lo")
        pv_mm, pv_read, xb_ready, xb_used = sem("pv_mm"), sem("pv_read"), sem("xb_ready"), sem("xb_used")
        y_normed = sem("y_normed")
        var_ready, rstd_ready = sem("var_ready"), sem("rstd_ready")
        turns = sem("turns")
        act_own, dve_own, pool_own = sem("act_own"), sem("dve_own"), sem("pool_own")
        l0_done, l1_done, l2_done = sem("l0_done"), sem("l1_done"), sem("l2_done")
        h1_done, h2_done = sem("h1_done"), sem("h2_done")
        conv_hi, conv_lo = sem("conv_hi"), sem("conv_lo")
        agg_mm, agg_hi, agg_lo = sem("agg_mm"), sem("agg_hi"), sem("agg_lo")
        wlb_ready = sem("wlb_ready")
        p1_mm, p1_hi, p1_lo, ex_ready = sem("p1_mm"), sem("p1_hi"), sem("p1_lo"), sem("ex_ready")
        w_exp, H_ready = sem("w_exp"), sem("H_ready")
        tm_ready, ef_ready, es_lo, e_used = sem("tm_ready"), sem("ef_ready"), sem("es_lo"), sem("e_used")
        g_mm, g_ev, gate_tanh, gate_ready = sem("g_mm"), sem("g_ev"), sem("gate_tanh"), sem("gate_ready")
        gated_ready, z_ready, sig_ready = sem("gated_ready"), sem("z_ready"), sem("sig_ready")
        dinv_ready, dsc_ready = sem("dinv_ready"), sem("dsc_ready")
        o2_mm, relu_ready, y2_ready = sem("o2_mm"), sem("relu_ready"), sem("y2_ready")
        h_mm, h_f, h_lo = sem("h_mm"), sem("h_f"), sem("h_lo")
        r_mm, r_copied, r_maxed = sem("r_mm"), sem("r_copied"), sem("r_maxed")
        tmax_ready, gmax_ready, scale_ready = sem("tmax_ready"), sem("gmax_ready"), sem("scale_ready")
        c3_hi, c3_lo = sem("c3_hi"), sem("c3_lo")
        o3_mm, o3_read, o_stored = sem("o3_mm"), sem("o3_read"), [sem(f"o_stored{u}") for u in range(2)]

        CREDITS = {"act": ((h_f, 2), (r_copied, 2), (relu_ready, TB)), "dve": ((h_lo, 2), (y2_ready, 2))}

        block = ctx.enter_context(nc.Block())

        ctx.enter_context(nc.allow_non_contiguous_dma(reason="a few columns of weights and biases"))

        @block.sync
        def _(sp):
            x_tiles = x_in.rearrange("(t p) d -> p t d", p=P)
            for c in range(B):
                sp.dma_start(x[:, TB * c:TB * c + TB, :], x_tiles[:, TB * c:TB * c + TB, :]).then_inc(x_landed[c], 16)
                if c == 0:
                    sp.dma_start(we[:, :, :], w_tiles(edge_in)).then_inc(w0_landed, 16)
                    sp.dma_start(w0x[:, :, 0:D], w_tiles(w0_in)).then_inc(w0_landed, 16)
                    sp.dma_start(w0x[:, :, D:D + 1], w_tiles(node_in)).then_inc(w0_landed, 16)
                    sp.dma_start(brow[:, :], vec_row(b0_in)).then_inc(w0_landed, 16)

            def load_adj(t):
                for k in range(2):
                    wait_from(sp, adj_cast, 2 * (t - 1) + k + 1)
                    sp.dma_start(adjf[:, k, :], adj_in[bass.ds(t * P, P), k * HALF:(k + 1) * HALF]) \
                        .then_inc(adj_landed[k], 16)

            sp.wait_ge(p0_lo, P0_GROUPS)
            load_adj(0)
            with sp.Fori(1, T) as t:
                load_adj(t)

            sp.wait_ge(adj_cast, 2 * T)
            sp.dma_start(wsx[:, :, 0:D], w_tiles(wsa_in)).then_inc(wt1_landed, 16)
            sp.dma_start(arow, asa_in.to_broadcast([P, 2 * D])).then_inc(wt1_landed, 16)
            sp.dma_start(wgx[:, :, 0:D], w_tiles(wg_in)).then_inc(wt1_landed, 16)
            for g, (w, b) in enumerate(((wa_in, ba_in), (wb_in, bb_in))):
                cols = w.rearrange("a (s k p) -> p s k a", s=2, p=P)
                sp.dma_start(wgx[:, :, D + g:D + g + 1], cols[:, 0, :, :]).then_inc(wt1_landed, 16)
                sp.dma_start(wsx[:, :, D + 2 + g:D + 3 + g], cols[:, 1, :, :]).then_inc(wt1_landed, 16)
            sp.wait_ge(l0_done, 4)
            for g, b in enumerate((ba_in, bb_in)):
                sp.dma_start(bab[:, 0, g:g + 1], vec_row(b)).then_inc(bias1_landed, 16)
            sp.dma_start(brow[:, :], vec_row(bg_in)).then_inc(bias1_landed, 16)

            sp.wait_ge(H_ready, 2)
            sp.dma_start(wlf[:, :, :], w_tiles(wl2_in)).then_inc(wt2_landed, 16)
            sp.wait_ge(l1_done, 4)
            sp.dma_start(W1f[:, :, :], w_tiles(W1_in)).then_inc(wh_landed, 16)
            sp.wait_ge(w_ready, 3)
            sp.dma_start(W2f[:, :, :], w_tiles(W2_in)).then_inc(wh_landed, 16)
            sp.dma_start(b1c[:, :], b1_in.rearrange("(k p) -> p k", p=P)).then_inc(wh_landed, 16)
            sp.dma_start(b2c[:, :], b2_in.rearrange("(k p) -> p k", p=P)).then_inc(wh_landed, 16)
            sp.dma_start(brow[:, :], vec_row(b3_in)).then_inc(wh_landed, 16)
            sp.wait_ge(h1_done, 4)
            sp.dma_start(W3f[:, :, :], w_tiles(W3_in)).then_inc(w3_landed, 16)

            with sp.Fori(0, T // 2) as i:
                for u in range(2):
                    sp.wait_ge(y_normed, 3 * T + 2 * i + u + 1)
                    sp.dma_start(out[bass.ds((2 * i + u) * P, P), :], ob[:, u, :]).then_inc(o_stored[u], 16)
            for u in range(2):
                sp.wait_ge(o_stored[u], 16 * (T // 2))

        @block.gpsimd
        def _(pool):
            own = Chain(pool, pool_own)
            for m in (ident, identb):
                own.link(nc.gpsimd.memset(m[:, :], 0.0))
                nc.gpsimd.affine_select(out=m[:, :], in_=m[:, :], compare_op=ALU.not_equal, fill=1.0, base=0,
                                        pattern=[[-1, P]], channel_multiplier=1).then_inc(const_ready, 1)
            own.link(nc.gpsimd.memset(epsc[:, :], EPS))
            own.link(nc.gpsimd.memset(ones[:, :], 1.0))
            own.link(nc.gpsimd.memset(mhalf[:, :], -0.5))
            nc.gpsimd.memset(w0x[:, :, D + 1:D + 2], 0.0).then_inc(const_ready, 1)

            def norm_factor(m, u):
                pool.wait_ge(var_ready, m + 1)
                own.link(nc.gpsimd.tensor_tensor(rstd[:, u, 0:1], mv[:, u, 1:2], epsc[:, :], ALU.add))
                nc.gpsimd.tensor_tensor(rstd[:, u, 1:2], rstd[:, u, 0:1], mhalf[:, 0:1], ALU.pow) \
                    .then_inc(rstd_ready, 1)

            def stage_h(t, u):
                wait_from(pool, e_mm, 2 * (t - 1))
                for part in (HI, LO):
                    nc.gpsimd.tensor_copy(hst[part][:, u, :, :],
                                          hT[part][:, :, bass.ds(t * P, P)].bitcast(F32)).then_inc(h_staged, 1)

            def bias_x(t, u, before=0):
                wait_from(pool, xb_used, before + t)
                nc.gpsimd.tensor_tensor(xb[:, u, :], tile(x, t), brow[:, :], ALU.add).then_inc(xb_ready, 1)

            pool.wait_ge(w0_landed, 64)
            for c in range(B):
                pool.wait_ge(x_landed[c], 16)
            pool.wait_ge(p0_lo, KD * (B + 1))
            stage_h(0, 0)
            stage_h(1, 1)
            pool.wait_ge(node_max, 1)
            nc.gpsimd.partition_all_reduce(nst[:, 1:2], nst[:, 0:1], P, RMAX).then_inc(node_gmax, 1)
            pool.wait_ge(node_exp, 1)
            nc.gpsimd.partition_all_reduce(nst[:, 4:5], nst[:, 3:4], P, RADD).then_inc(node_sum, 1)
            bias_x(0, 0)
            with pool.Fori(0, T // 2 - 1) as i:
                own.enter(i, 2)
                for u in range(2):
                    stage_h(2 * i + 2 + u, u)
                    bias_x(2 * i + 1 + u, 1 - u)
                    norm_factor(2 * i + u, u)
            own.leave(T // 2 - 1)
            bias_x(T - 1, 1)
            norm_factor(T - 2, 0)
            norm_factor(T - 1, 1)
            pool.drain().then_inc(l0_done, 1)

            pool.wait_ge(l0_done, 4)
            own.link(nc.gpsimd.tensor_tensor(dinv[:, :], deg[:, :, 0], deg[:, :, 1], ALU.add))
            own.link(nc.gpsimd.tensor_tensor(dinv[:, :], dinv[:, :], ones[:, :], ALU.add))
            nc.gpsimd.tensor_tensor(dinv[:, :], dinv[:, :], mhalf[:, :], ALU.pow).then_inc(dinv_ready, 1)
            for t in range(T):
                nc.gpsimd.tensor_scalar(x16[:, HI, t, :], x[:, t, :], XS, None, ALU.mult).then_inc(conv_hi, 1)
            pool.wait_ge(w_ready, 2)
            for part in (HI, LO):
                nc.gpsimd.tensor_copy(wlb[part][:, :, :],
                                      wss[part][:, :, D + 1:D + 2].bitcast(F32).to_broadcast([P, KD, P])) \
                    .then_inc(wlb_ready, 1)

            with pool.Fori(0, B) as b:
                own.enter(b, TB)
                for k in range(TB):
                    norm_factor(T + b * TB + k, k % 2)
            own.leave(B)
            pool.drain().then_inc(l1_done, 1)

            pool.wait_ge(l1_done, 4)
            with pool.Fori(0, T // 2) as i:
                own.enter(i, 2)
                for u in range(2):
                    norm_factor(2 * T + 2 * i + u, u)
            own.leave(T // 2)
            pool.drain().then_inc(l2_done, 1)

            pool.wait_ge(l2_done, 4)
            pool.drain().then_inc(h1_done, 1)
            pool.wait_ge(tmax_ready, 1)
            nc.gpsimd.partition_all_reduce(g1[:, 1:2], g1[:, 0:1], P, RMAX).then_inc(gmax_ready, 1)
            pool.wait_ge(h1_done, 4)
            pool.wait_ge(w3_landed, 16)
            own.link(nc.gpsimd.tensor_copy(W3s[HI][:, :, :], W3f[:, :, :]))
            nc.gpsimd.tensor_tensor(W3s[LO][:, :, :], W3f[:, :, :], W3s[HI][:, :, :].bitcast(F32), ALU.subtract) \
                .then_inc(wp_ready, 1)
            pool.drain().then_inc(h2_done, 1)
            pool.wait_ge(tmax_ready, 2)
            nc.gpsimd.partition_all_reduce(g1[:, 1:2], g1[:, 0:1], P, RMAX).then_inc(gmax_ready, 1)

            bias_x(0, 0, T)
            bias_x(1, 1, T)
            with pool.Fori(0, T // 2 - 1) as i:
                own.enter(i, 2)
                for u in range(2):
                    norm_factor(3 * T + 2 * i + u, u)
                    bias_x(2 * i + 2 + u, u, T)
            own.leave(T // 2 - 1)
            for u in range(2):
                norm_factor(4 * T - 2 + u, u)

        @block.tensor
        def _(pe):
            mm = nc.tensor.matmul

            def project(to, s, cols, w, width, tiles=None):
                tiles = tiles or range(KD)
                for k in tiles:
                    for a, b in ((HI, HI), (HI, LO), (LO, HI)):
                        ins = mm(to, s[a][:, k, cols], w[b][:, k, 0:width],
                                 start=(k == 0 and (a, b) == (HI, HI)),
                                 stop=(k == tiles[-1] and a == LO))
                return ins

            pe.wait_ge(const_ready, 3)
            for n in range(P0_GROUPS):
                if n >= 4:
                    pe.wait_ge(p0_lo, n - 3)
                to = 4 + n % 4
                if n < 2 * B:
                    b, f = n // KD, n % KD
                    pe.wait_ge(x_landed[b], 16)
                    for k in range(TB):
                        ins = nc.tensor.transpose(ps[:, to, k * P:(k + 1) * P],
                                                  x[:, b * TB + k, f * P:(f + 1) * P], ident[:, :])
                elif n < 4 * B:
                    b, o = (n - 2 * B) // KD, n % KD
                    pe.wait_ge(p0_lo, 2 * (b + 1))
                    if n == 2 * B:
                        pe.wait_ge(w_ready, 1)
                    for k in range(KD):
                        for p, q in ((HI, HI), (HI, LO), (LO, HI)):
                            ins = mm(bank(to), wes[p][:, k, o * P:(o + 1) * P], xT0[q][:, k, b * CB:(b + 1) * CB],
                                     start=(k == 0 and (p, q) == (HI, HI)), stop=(k == KD - 1 and p == LO))
                else:
                    t = n - 4 * B
                    ins = project(bank(to, D + 2), xT0, slice(t * P, (t + 1) * P), w0s, D + 2)
                ins.then_inc(p0_mm, 1)

            def scores(t, u, banks):
                pe.wait_ge(h_staged, 2 * (t + 1))
                for c in banks:
                    if c % 2 == 0:
                        wait_from(pe, e_read, 2 * (t - 1) + c // 2 + 1)
                    for k in range(KD):
                        for p, q in ((HI, HI), (HI, LO), (LO, HI)):
                            ins = mm(bank(c), hst[p][:, u, k, :], hT[q][:, k, c * CB:(c + 1) * CB],
                                     start=(k == 0 and (p, q) == (HI, HI)), stop=(k == KD - 1 and p == LO))
                    if c % 2:
                        ins.then_inc(e_mm, 1)

            def adj_transpose(t, k):
                pe.wait_ge(adj_cast, 2 * t + k + 1)
                wait_from(pe, adj_ev[1 - k], t + k)
                to = ps[:, 6, :].bitcast(BF16)
                for j in range(T // 2):
                    c = k * HALF + j * P
                    ins = nc.tensor.transpose(to[:, j * P:(j + 1) * P], adjb[:, c:c + P], identb[:, :])
                ins.then_inc(adj_tr, 1)

            def weighted(t, u, between=lambda: None, after=lambda: None):
                def turn(g):
                    n = t * TB + g
                    if g == 0:
                        pe.wait_ge(exp_done, t + 1)
                    wait_from(pe, pt_lo, n - 1)
                    for j in range(4):
                        jt = 4 * g + j
                        ins = nc.tensor.transpose(ps[:, 4 + g % 2, j * P:(j + 1) * P],
                                                  em[:, u, jt * P:(jt + 1) * P], ident[:, :])
                    ins.then_inc(pt_tr, 1)

                def times(g):
                    pe.wait_ge(pt_lo, t * TB + g + 1)
                    if g == 0:
                        wait_from(pe, pv_read, t)
                    for j in range(4):
                        jt = 4 * g + j
                        for part in ((HI, LO) if jt == 0 else (LO, HI)):
                            if part == HI:
                                ins = mm(bank(7), PT[HI][:, jt, :], sup[:, jt, :], start=(jt == 0),
                                         stop=(jt == T - 1))
                            else:
                                ins = mm(bank(7, D), PT[LO][:, jt, :], sup[:, jt, 0:D], start=False, stop=False,
                                         skip_group_check=True)
                    return ins

                turn(0)
                turn(1)
                between()
                times(0)
                turn(2)
                times(1)
                turn(3)
                times(2)
                after()
                times(3).then_inc(pv_mm, 1)

            def round0(t, u):
                if isinstance(t, int) and t == 0:
                    scores(t, u, range(B))
                    adj_transpose(t, 0)
                    adj_transpose(t, 1)
                    return
                scores(t, u, range(B - 1))

                def between():
                    scores(t, u, (B - 1,))
                    adj_transpose(t, 0)

                weighted(t - 1, 1 - u, between, lambda: adj_transpose(t, 1))

            round0(0, 0)
            round0(1, 1)
            with pe.Fori(0, T // 2 - 1) as i:
                for u in range(2):
                    round0(2 * i + 2 + u, u)
            weighted(T - 1, 1)
            pe.drain().then_inc(l0_done, 1)

            pe.wait_ge(l0_done, 4)
            for n in range(P1_GROUPS):
                if n >= 4:
                    pe.wait_ge(p1_hi, n - 3)
                    pe.wait_ge(p1_lo, min(n - 3, P1_SPLITS))
                to = n % 4
                if n < 2 * B:
                    b, f = n // KD, n % KD
                    for k in range(TB):
                        ins = nc.tensor.transpose(ps[:, to, k * P:(k + 1) * P],
                                                  x[:, b * TB + k, f * P:(f + 1) * P], ident[:, :])
                elif n < P1_SPLITS:
                    t = n - 2 * B
                    if t == 0:
                        pe.wait_ge(w_ready, 2)
                        pe.wait_ge(p1_lo, 2 * B)
                    ins = project(bank(to, D + 4), xT1, slice(t * P, (t + 1) * P), wss, D + 4)
                else:
                    b = n - P1_SPLITS
                    if b == 0:
                        pe.wait_ge(wlb_ready, 2)
                    for k in range(KD):
                        for p, q in ((HI, HI), (HI, LO), (LO, HI)):
                            ins = mm(bank(to), wlb[p][:, k, :], xT1[q][:, k, b * CB:(b + 1) * CB],
                                     start=(k == 0 and (p, q) == (HI, HI)), stop=(k == KD - 1 and p == LO))
                ins.then_inc(p1_mm, 1)

            def aggregate_tiles(layer, b, f, jts, diag=False):
                for jt in jts:
                    if jt == 0:
                        wait_from(pe, agg_lo, (layer * B + b) * KD + f - 1)
                    if f == 0 and isinstance(b, int) and b == 0:
                        pe.wait_ge(conv_lo, layer * T + jt + 1)
                    for part in (HI, LO):
                        ins = mm(bank(4 + f), x16[:, part, jt, f * P:(f + 1) * P],
                                 adjT[:, jt, bass.ds(b * CB, CB)], start=(jt == 0 and part == HI),
                                 stop=(jt == T - 1 and part == LO))
                    if diag and jt == 0:
                        if isinstance(b, int) and b == 0:
                            pe.wait_ge(conv_lo, layer * T + TB)
                        for k in range(TB):
                            for part in (HI, LO):
                                mm(ps[:, 4 + f, k * P:(k + 1) * P],
                                   tile(x16[:, part, :, f * P:(f + 1) * P], b * TB + k),
                                   identb[:, :], start=False, stop=False, skip_group_check=True)
                    if jt == T - 1:
                        ins.then_inc(agg_mm, 1)

            def aggregate(layer, b, f, diag=False):
                aggregate_tiles(layer, b, f, range(T), diag)

            def attend(b, pair):
                pe.wait_ge(es_lo, b * PAIRS + pair + 1)
                if pair == 0:
                    wait_from(pe, z_ready, b * TB)
                for jt in (2 * pair, 2 * pair + 1):
                    for k in range(TB):
                        for p, q in ((HI, HI), (HI, LO), (LO, HI)):
                            ins = mm(bank(k, D + 2), es[p][:, jt % RE, k * P:(k + 1) * P], H[q][:, jt, :],
                                     start=(jt == 0 and (p, q) == (HI, HI)), stop=(jt == T - 1 and p == LO))
                ins.then_inc(e_used, 1)

            def neighbours(b):
                pe.wait_ge(agg_lo, (b + 1) * KD)
                for k in range(TB):
                    project(bank(G_BANK[k], D + 2), agg, slice(k * P, (k + 1) * P), wgs, D + 2).then_inc(g_mm, 1)

            def block1(b):
                first = 0
                wait_from(pe, g_ev, b * TB)
                for pair in range(PAIRS):
                    if pair < len(AGG_TILES):
                        for jt in range(first, first + AGG_TILES[pair]):
                            for f in range(KD):
                                aggregate_tiles(0, b, f, (jt,))
                        first += AGG_TILES[pair]
                    attend(b, pair)
                    if pair == len(AGG_TILES) - 1:
                        neighbours(b)

            pe.wait_ge(H_ready, 2)
            block1(0)
            with pe.Fori(1, B) as b:
                block1(b)
            pe.drain().then_inc(l1_done, 1)

            def out2(b):
                pe.wait_ge(w_ready, 3)
                for k in range(TB):
                    if k == 0:
                        pe.wait_ge(agg_lo, (B + b + 1) * KD)
                    pe.wait_ge(relu_ready, TB + (b - 1) * TB + k + 1)
                    project(bank(k, D), agg, slice(k * P, (k + 1) * P), wls, D).then_inc(o2_mm, 1)

            for jt in range(T):
                for f in range(KD):
                    aggregate_tiles(1, 0, f, (jt,), diag=True)
            with pe.Fori(1, B) as b:
                aggregate(1, b, 0, diag=True)
                out2(b - 1)
                aggregate(1, b, 1, diag=True)
            out2(B - 1)
            pe.drain().then_inc(l2_done, 1)

            def hidden1(b):
                pe.wait_ge(agg_lo, (2 * B + b + 1) * KD)
                for o in range(KH):
                    pe.wait_ge(h_f, 2 + b * KH + o - 1)
                    for k in range(KD):
                        for p, q in ((HI, HI), (HI, LO), (LO, HI)):
                            ins = mm(bank(o % 2), W1s[p][:, k, o * P:(o + 1) * P], agg[q][:, k, :],
                                     start=(k == 0 and (p, q) == (HI, HI)), stop=(k == KD - 1 and p == LO))
                    ins.then_inc(h_mm, 1)

            def rows(b, ws, width):
                for k in range(TB):
                    n = b * TB + k
                    pe.wait_ge(r_copied, 2 + n - 1)
                    for o in range(KH):
                        if k == 0:
                            pe.wait_ge(h_lo, 2 + b * KH + o + 1)
                        for p, q in ((HI, HI), (HI, LO), (LO, HI)):
                            ins = mm(bank(2 + k % 2, width), hh[p][:, o, k * P:(k + 1) * P], ws[q][:, o, :],
                                     start=(o == 0 and (p, q) == (HI, HI)), stop=(o == KH - 1 and p == LO))
                    ins.then_inc(r_mm, 1)

            for jt in range(T):
                for f in range(KD):
                    aggregate_tiles(2, 0, f, (jt,))
            pe.wait_ge(wp_ready, 2)
            with pe.Fori(1, B) as b:
                aggregate(2, b, 0)
                hidden1(b - 1)
                rows(b - 1, W2s, HID)
                aggregate(2, b, 1)
            hidden1(B - 1)
            rows(B - 1, W2s, HID)
            pe.drain().then_inc(h1_done, 1)

            def hidden2(b, o):
                pe.wait_ge(h_f, 2 + (B + b - 1) * KH + o + 1)
                for jt in range(T):
                    for part in (HI, LO):
                        ins = mm(bank(4 + o), g16(jt, part, o * P, P), adjT[:, jt, bass.ds(b * CB, CB)],
                                 start=(jt == 0 and part == HI), stop=(jt == T - 1 and part == LO))
                ins.then_inc(h_mm, 1)

            for jt in range(T):
                pe.wait_ge(c3_lo, jt + 1)
                for o in range(KH):
                    for part in (HI, LO):
                        ins = mm(bank(4 + o), g16(jt, part, o * P, P), adjT[:, jt, 0:CB],
                                 start=(jt == 0 and part == HI), stop=(jt == T - 1 and part == LO))
                    if jt == T - 1:
                        ins.then_inc(h_mm, 1)
            pe.wait_ge(wp_ready, 3)
            with pe.Fori(1, B) as b:
                hidden2(b, 0)
                rows(B + b - 1, W3s, D)
                for o in range(1, KH):
                    hidden2(b, o)
            rows(2 * B - 1, W3s, D)
            pe.drain().then_inc(h2_done, 1)

            def out3(t, u):
                wait_from(pe, o3_read, t - 1)
                for jt in range(T):
                    if isinstance(t, int) and t == 0:
                        pe.wait_ge(c3_lo, T + jt + 1)
                    ins = mm(bank(u), adjT[:, jt, bass.ds(t * P, P)], f16[:, jt, :], start=(jt == 0),
                             stop=(jt == T - 1))
                ins.then_inc(o3_mm, 1)

            out3(0, 0)
            out3(1, 1)
            with pe.Fori(1, T // 2) as i:
                for u in range(2):
                    out3(2 * i + u, u)

        @block.scalar
        def _(act):
            own = Chain(act, act_own)
            for s, n in CREDITS["act"]:
                act.sem_inc(s, n)
            run = nc.scalar.activation

            for n in range(P0_GROUPS):
                act.wait_ge(p0_mm, n + 1)
                b, f, t = n // KD % B, n % KD, n - 4 * B
                to = (xT0[HI][:, f, b * CB:(b + 1) * CB] if n < 2 * B else
                      hT[HI][:, f, b * CB:(b + 1) * CB] if n < 4 * B else sup[:, t, 0:D])
                run(to, bank(4 + n % 4, CB if n < 4 * B else D), ACT.Copy).then_inc(p0_hi, 1)

            def cast(t):
                for k in range(2):
                    act.wait_ge(adj_landed[k], 16 * (t + 1))
                    wait_from(act, adj_tr, 2 * (t - 1) + k + 1)
                    wait_from(act, fill_ready, t)
                    run(adjb[:, k * HALF:(k + 1) * HALF], adjf[:, k, :], ACT.Copy,
                        accum_out=tile(deg, t)[:, k:k + 1]).then_inc(adj_cast, 1)

            def pt_high(t, g):
                act.wait_ge(pt_tr, t * TB + g + 1)
                run(PT[HI][:, 4 * g:4 * g + 4, :], bank(4 + g % 2).rearrange("p (a b) -> p a b", b=P), ACT.Copy) \
                    .then_inc(pt_hi, 1)

            def round0(t, u, more=True):
                if not (isinstance(t, int) and t == 0):
                    for g in range(4):
                        pt_high(t - 1, g)
                act.wait_ge(e_maxed, t + 1)
                wait_from(act, pv_read, t - 1)
                run(em[:, u, :], em[:, u, :], ACT.Exp, bias=negm[:, u:u + 1], accum_out=Z[:, u:u + 1]) \
                    .then_inc(exp_done, 1)
                act.wait_ge(adj_tr, 2 * t + 2)
                run(adjT[:, T // 2:T, bass.ds(t * P, P)],
                    ps[:, 6, :].bitcast(BF16).rearrange("p (a b) -> p a b", b=P), ACT.Copy).then_inc(adj_ev[1], 1)
                if more:
                    cast(t + 1)

            cast(0)
            act.wait_ge(node_neg, 1)
            run(nl[:, :], nl[:, :], ACT.Exp, bias=nst[:, 2:3], accum_out=nst[:, 3:4]).then_inc(node_exp, 1)
            round0(0, 0)
            round0(1, 1)
            with act.Fori(1, T // 2 - 1) as i:
                for u in range(2):
                    round0(2 * i + u, u)
            round0(T - 2, 0)
            round0(T - 1, 1, more=False)
            for g in range(4):
                pt_high(T - 1, g)
            act.drain().then_inc(l0_done, 1)

            act.wait_ge(l0_done, 4)
            for n in range(P1_GROUPS):
                act.wait_ge(p1_mm, n + 1)
                b, f, t = n // KD, n % KD, n - 2 * B
                if n < 2 * B:
                    run(xT1[HI][:, f, b * CB:(b + 1) * CB], bank(n % 4), ACT.Copy).then_inc(p1_hi, 1)
                elif n < P1_SPLITS:
                    own.link(run(vj[:, t, :], ps[:, n % 4, D:D + 1], ACT.Exp, scale=-SLOPE))
                    run(H[HI][:, t, 0:D], bank(n % 4, D), ACT.Copy, scale=vj[:, t, :]).then_inc(p1_hi, 1)
                else:
                    b = n - P1_SPLITS
                    run(slrow[:, b * CB:(b + 1) * CB], bank(n % 4), ACT.Copy).then_inc(p1_hi, 1)
            run(H[HI][:, :, D:D + 1], vj[:, :, :], ACT.Copy).then_inc(H_ready, 1)
            act.wait_ge(ex_ready, 1)
            run(wi[:, :], ex[:, :, 1], ACT.Exp, scale=SLOPE).then_inc(w_exp, 1)

            def agg_high(layer, b, f):
                act.wait_ge(agg_mm, (layer * B + b) * KD + f + 1)
                run(agg[HI][:, f, :], bank(4 + f), ACT.Copy, scale=1.0 / XS).then_inc(agg_hi, 1)

            def edge_exp(b, pair):
                n, s = b * PAIRS + pair, slice(2 * pair % RE, 2 * pair % RE + 2)
                act.wait_ge(tm_ready, 2 * (n + 1))
                wait_from(act, e_used, n + 1 - RE // 2)
                run(es[HI][:, s, :], tm[:, s, :], ACT.Exp, scale=SLOPE - 1.0)
                wait_from(act, es_lo, n + 1 - RE // 2)
                run(ef[:, s, :], tm[:, s, :], ACT.Exp, scale=SLOPE - 1.0).then_inc(ef_ready, 1)

            def gates(b):
                act.wait_ge(g_ev, (b + 1) * TB)
                run(gate[:, :, :], gate[:, :, :], ACT.Tanh, scale=0.5).then_inc(gate_tanh, 1)

            def gated(b):
                act.wait_ge(gate_ready, b + 1)
                for k in range(TB):
                    run(g4[:, k, :], g4[:, k, :], ACT.Copy, scale=gate[:, k, 1:2]).then_inc(gated_ready, 1)

            def sigmoid(b, k):
                m = b * TB + k
                act.wait_ge(z_ready, m + 1)
                own.link(run(z[:, k, :], z[:, k, :], ACT.Tanh, scale=0.5))
                act.wait_ge(y_normed, T + m - 1)
                run(y[:, k % 2, :], z[:, k, :], ACT.Copy, scale=0.5, bias=0.5).then_inc(sig_ready, 1)

            def block1(b):
                for pair in range(2, PAIRS):
                    if not (isinstance(b, int) and b == 0) and pair - 2 < TB:
                        sigmoid(b - 1, pair - 2)
                    edge_exp(b, pair)
                    if pair == 6:
                        for f in range(KD):
                            agg_high(0, b, f)
                gates(b)
                if not (isinstance(b, int) and b == B - 1):
                    edge_exp(b + 1, 0)
                gated(b)
                if not (isinstance(b, int) and b == B - 1):
                    edge_exp(b + 1, 1)

            act.wait_ge(p1_lo, P1_SPLITS)
            edge_exp(0, 0)
            edge_exp(0, 1)
            block1(0)
            with act.Fori(1, B - 1) as b:
                own.enter(b - 1, TB)
                block1(b)
            own.leave(B - 2)
            block1(B - 1)

            def conv_high(layer, t, scale):
                if t >= T - TB:
                    act.wait_ge(y_normed, layer * T + t + 1)
                run(x16[:, HI, t, :], x[:, t, :], ACT.Copy, scale=scale).then_inc(conv_hi, 1)

            act.wait_ge(agg_mm, B * KD)
            act.wait_ge(dsc_ready, 1)
            for t in range(T):
                if t >= 4 and t % 2 == 0 and t // 2 - 2 < TB:
                    sigmoid(B - 1, t // 2 - 2)
                conv_high(1, t, dsc[:, t:t + 1])
            act.drain().then_inc(l1_done, 1)

            def relu2(b, tiles=range(TB)):
                for k in tiles:
                    n = b * TB + k
                    act.wait_ge(o2_mm, n + 1)
                    act.wait_ge(y2_ready, 2 + n - 1)
                    run(xb[:, k % 2, :], bank(k, D), ACT.Relu, scale=dinv[:, bass.ds(n, 1)]).then_inc(relu_ready, 1)

            agg_high(1, 0, 0)
            with act.Fori(1, B) as b:
                agg_high(1, b - 1, 1)
                relu2(b - 1)
                agg_high(1, b, 0)
            agg_high(1, B - 1, 1)
            act.wait_ge(agg_mm, 2 * B * KD)
            for k in range(TB):
                relu2(B - 1, (k,))
                for t in range(3 * k, 3 * k + 3):
                    conv_high(2, t, XS)
            for t in range(T - TB, T):
                conv_high(2, t, XS)
            act.wait_ge(wh_landed, 80)
            for f, s in ((W1f[:, :, :], W1s), (W2f, W2s)):
                run(s[HI][:, :, :], f, ACT.Copy).then_inc(wp_hi, 1)
            act.drain().then_inc(l2_done, 1)

            act.wait_ge(l2_done, 4)
            act.wait_ge(wh_landed, 80)

            def hidden(b, o, frm, bias, scale):
                n = b * KH + o
                act.wait_ge(h_mm, n + 1)
                run(hh[HI][:, o, :], bank(frm), ACT.Relu, bias=bias[:, o:o + 1], scale=scale)
                act.wait_ge(h_lo, 2 + n - 1)
                run(hf[:, o % 2, :], bank(frm), ACT.Relu, bias=bias[:, o:o + 1], scale=scale).then_inc(h_f, 1)

            def rows(b, to, first, width):
                for k in range(TB):
                    act.wait_ge(r_mm, b * TB + k + 1)
                    run(tile(to, b * TB + k + first), bank(2 + k % 2, width), ACT.Copy).then_inc(r_copied, 1)

            def mid(b):
                for o in range(KH):
                    hidden(b, o, o % 2, b1c, 1.0)
                rows(b, G, AHEAD, HID)

            agg_high(2, 0, 0)
            with act.Fori(1, B) as b:
                agg_high(2, b - 1, 1)
                mid(b - 1)
                agg_high(2, b, 0)
            agg_high(2, B - 1, 1)
            mid(B - 1)
            act.drain().then_inc(h1_done, 1)

            act.wait_ge(scale_ready, 1)
            for t in range(T):
                wait_from(act, c3_lo, t - AHEAD + 1)
                run(g16(t, HI), G[:, t + AHEAD, :], ACT.Copy, scale=g1[:, 2:3]).then_inc(c3_hi, 1)
            act.wait_ge(h1_done, 4)
            for o in range(KH):
                hidden(B, o, 4 + o, b2c, g1[:, 3:4])
            with act.Fori(1, B) as b:
                rows(B + b - 1, F, -B * TB, D)
                for o in range(KH):
                    hidden(B + b, o, 4 + o, b2c, g1[:, 3:4])
            rows(2 * B - 1, F, -B * TB, D)
            act.drain().then_inc(h2_done, 1)

            act.wait_ge(scale_ready, 2)
            for t in range(T):
                run(f16[:, t, 0:D], F[:, t, :], ACT.Copy, scale=g1[:, 2:3]).then_inc(c3_hi, 1)

        @block.vector
        def _(dve):
            own = Chain(dve, dve_own)
            for s, n in CREDITS["dve"]:
                dve.sem_inc(s, n)
            tt, stt, ts = nc.vector.tensor_tensor, nc.vector.scalar_tensor_tensor, nc.vector.tensor_scalar

            def split(full, parts):
                own.link(nc.vector.tensor_copy(parts[HI][:, :, :], full))
                own.link(tt(parts[LO][:, :, :], full, parts[HI][:, :, :].bitcast(F32), ALU.subtract))

            def low(to, frm, high):
                return tt(to, frm, high.bitcast(F32), ALU.subtract)

            def normed(m, u, to):
                dve.wait_ge(rstd_ready, m + 1)
                ts(to, y[:, u, :], mv[:, u, 0:1], rstd[:, u, 1:2], ALU.subtract, ALU.mult).then_inc(y_normed, 1)

            def y_free(m):
                dve.wait_ge(y_normed, m - 1)

            def moments(u):
                own.link(nc.vector.bn_stats(stats[:, u, :], y[:, u, :]))
                pause(dve, turns)
                nc.vector.bn_aggr(mv[:, u, :], stats[:, u, :]).then_inc(var_ready, 1)

            dve.wait_ge(w0_landed, 64)
            dve.wait_ge(const_ready, 3)
            split(we[:, :, :], wes)
            own.link(nc.vector.tensor_copy(w0s[HI][:, :, :], w0x[:, :, :]))
            low(w0s[LO][:, :, :], w0x[:, :, :], w0s[HI][:, :, :]).then_inc(w_ready, 1)
            for n in range(P0_GROUPS):
                dve.wait_ge(p0_hi, n + 1)
                b, f, t = n // KD % B, n % KD, n - 4 * B
                if n < 4 * B:
                    s = xT0 if n < 2 * B else hT
                    cols = slice(b * CB, (b + 1) * CB)
                    low(s[LO][:, f, cols], bank(4 + n % 4), s[HI][:, f, cols]).then_inc(p0_lo, 1)
                else:
                    own.link(nc.vector.tensor_copy(nl[:, t:t + 1], ps[:, 4 + n % 4, D:D + 1]))
                    low(sup[:, t, D:2 * D], bank(4 + n % 4, D), sup[:, t, 0:D]).then_inc(p0_lo, 1)
            nc.vector.reduce_max(nst[:, 0:1], nl[:, :], AX_X).then_inc(node_max, 1)
            dve.wait_ge(node_gmax, 1)
            ts(nst[:, 2:3], nst[:, 1:2], -1.0, None, ALU.mult).then_inc(node_neg, 1)

            def masked_max(t, u, h):
                dve.wait_ge(e_mm, 2 * t + h + 1)
                wait_from(dve, pv_mm, t - 1)
                pause(dve, turns)
                banks = ps[:, 2 * h:2 * h + 2, :].rearrange("p a b -> p (a b)")
                cols = slice(h * HALF, (h + 1) * HALF)
                nc.vector.tensor_tensor_reduce(out=em[:, u, cols], in0=banks, in1=fill[:, cols], scale=1.0,
                                               scalar=-3.0e38, op0=ALU.add, op1=ALU.max,
                                               accum_out=mx[:, u, h:h + 1]).then_inc(e_read, 1)

            def pt_low(t, g):
                dve.wait_ge(pt_hi, t * TB + g + 1)
                c = slice(4 * g, 4 * g + 4)
                low(PT[LO][:, c, :], bank(4 + g % 2).rearrange("p (a b) -> p a b", b=P), PT[HI][:, c, :]) \
                    .then_inc(pt_lo, 1)

            def final0(t, u):
                dve.wait_ge(exp_done, t + 1)
                own.link(ts(rowf[:, u, 0:1], negm[:, u:u + 1], BIG / 2, nl[:, bass.ds(t, 1)], ALU.is_lt, ALU.mult))
                own.link(nc.vector.reciprocal(rowf[:, u, 1:2], Z[:, u:u + 1]))
                own.link(tt(rowf[:, u, 2:3], rowf[:, u, 0:1], rowf[:, u, 1:2], ALU.mult))
                dve.wait_ge(pv_mm, t + 1)
                dve.wait_ge(xb_ready, t + 1)
                stt(y[:, u, :], bank(7, D), rowf[:, u, 2:3], xb[:, u, :], ALU.mult, ALU.add).then_inc(xb_used, 1)
                dve.wait_ge(xb_used, t + 1)
                stt(y[:, u, :], ps[:, 7, D:2 * D], rowf[:, u, 2:3], y[:, u, :], ALU.mult, ALU.add) \
                    .then_inc(pv_read, 1)
                dve.wait_ge(pv_read, t + 1)
                moments(u)

            def round0(t, u):
                first = isinstance(t, int) and t == 0
                if not (isinstance(t, int) and t < 2):
                    normed(t - 2, u, tile(x, t - 2))
                dve.wait_ge(adj_cast, 2 * t + 2)
                ts(fill[:, :], adjb[:, :], -1.0, BIG, ALU.add, ALU.mult).then_inc(fill_ready, 1)
                dve.wait_ge(fill_ready, t + 1)
                masked_max(t, u, 0)
                if not first:
                    pt_low(t - 1, 0)
                    pt_low(t - 1, 1)
                masked_max(t, u, 1)
                dve.wait_ge(e_read, 2 * t + 2)
                ts(negm[:, u:u + 1], mx[:, u, 0:1], mx[:, u, 1:2], -1.0, ALU.max, ALU.mult).then_inc(e_maxed, 1)
                if not first:
                    pt_low(t - 1, 2)
                dve.wait_ge(adj_tr, 2 * t + 1)
                nc.vector.tensor_copy(adjT[:, 0:T // 2, bass.ds(t * P, P)],
                                      ps[:, 6, :].bitcast(BF16).rearrange("p (a b) -> p a b", b=P)) \
                    .then_inc(adj_ev[0], 1)
                if not first:
                    pt_low(t - 1, 3)
                    final0(t - 1, 1 - u)

            LINKS0 = 4
            round0(0, 0)
            dve.wait_ge(node_sum, 1)
            own.link(nc.vector.reciprocal(nst[:, 3:4], nst[:, 4:5]))
            own.link(ts(nl[:, :], nl[:, :], nst[:, 3:4], None, ALU.mult))
            round0(1, 1)
            with dve.Fori(0, T // 2 - 1) as i:
                own.enter(i, 2 * LINKS0)
                for u in range(2):
                    round0(2 * i + 2 + u, u)
            own.leave(T // 2 - 1)
            normed(T - 2, 0, x[:, T - 2, :])
            for g in range(4):
                pt_low(T - 1, g)
            dve.wait_ge(wt1_landed, 7 * 16)
            for k in range(KD):
                for g, c in ((0, D), (1, 0)):
                    own.link(nc.vector.tensor_tensor_reduce(
                        out=scr, in0=wsx[:, k, 0:D], in1=arow[:, c:c + D], scale=1.0, scalar=0.0,
                        op0=ALU.mult, op1=ALU.add, accum_out=wsx[:, k, D + g:D + g + 1]))
            final0(T - 1, 1)
            normed(T - 1, 1, x[:, T - 1, :])
            dve.drain().then_inc(l0_done, 1)

            dve.wait_ge(l0_done, 4)
            for n in range(2 * B):
                b, f = n // KD, n % KD
                cols = slice(b * CB, (b + 1) * CB)
                dve.wait_ge(p1_hi, n + 1)
                low(xT1[LO][:, f, cols], bank(n % 4), xT1[HI][:, f, cols]).then_inc(p1_lo, 1)
            own.link(nc.vector.tensor_copy(wss[HI][:, :, :], wsx))
            low(wss[LO][:, :, :], wsx, wss[HI][:, :, :]).then_inc(w_ready, 1)
            for n in range(2 * B, P1_SPLITS):
                t = n - 2 * B
                dve.wait_ge(p1_hi, n + 1)
                own.link(nc.vector.tensor_copy(ex[:, t, :], ps[:, n % 4, D:D + 4]))
                stt(H[LO][:, t, 0:D], bank(n % 4, D), vj[:, t, :], H[HI][:, t, 0:D].bitcast(F32),
                    ALU.mult, ALU.subtract).then_inc(p1_lo, 1)
                dve.wait_ge(conv_hi, t + 1)
                stt(x16[:, LO, t, :], x[:, t, :], XS, x16[:, HI, t, :], ALU.mult, ALU.subtract) \
                    .then_inc(conv_lo, 1)
            split(wgx, wgs)
            dve.wait_ge(bias1_landed, 48)
            own.link(tt(ex[:, :, 2:4], ex[:, :, 2:4], bab[:, :, :].to_broadcast([P, T, 2]), ALU.add))
            dve.sem_inc(ex_ready, 1)
            for part in (HI, LO):
                own.link(nc.vector.memset(H[part][:, :, D + 1:D + 2].bitcast(F32), 0.0))
            dve.wait_ge(H_ready, 1)
            low(H[LO][:, :, D:D + 1], vj[:, :, :], H[HI][:, :, D:D + 1]).then_inc(H_ready, 1)
            dve.wait_ge(dinv_ready, 1)
            ts(dsc[:, :], dinv[:, :], XS, None, ALU.mult).then_inc(dsc_ready, 1)
            dve.wait_ge(w_exp, 1)
            own.link(ts(wi[:, :], wi[:, :], EPS, None, ALU.mult))
            dve.wait_ge(p1_mm, P1_GROUPS)
            dve.wait_ge(p1_hi, P1_GROUPS)

            def agg_low(layer, b, f):
                dve.wait_ge(agg_hi, (layer * B + b) * KD + f + 1)
                stt(agg[LO][:, f, :], bank(4 + f), 1.0 / XS, agg[HI][:, f, :].bitcast(F32),
                    ALU.mult, ALU.subtract).then_inc(agg_lo, 1)

            def edge_scores(b, pair):
                j0 = 2 * pair
                own.link(ts(nb[:, :, :], adjT[:, j0:j0 + 2, bass.ds(b * CB, CB)], -1.0, -FAR, ALU.add, ALU.mult))
                wait_from(dve, ef_ready, b * PAIRS + pair + 1 - RE // 2)
                for jt in (j0, j0 + 1):
                    stt(tm[:, jt % RE, :], slrow[:, bass.ds(b * CB, CB)], ex[:, jt, 0:1], nb[:, jt % 2, :],
                        ALU.add, ALU.max).then_inc(tm_ready, 1)
                dve.wait_ge(tm_ready, 2 * (b * PAIRS + pair + 1))

            def edge_low(b, pair):
                n, s = b * PAIRS + pair, slice(2 * pair % RE, 2 * pair % RE + 2)
                dve.wait_ge(ef_ready, n + 1)
                wait_from(dve, e_used, n + 1 - RE // 2)
                low(es[LO][:, s, :], ef[:, s, :], es[HI][:, s, :]).then_inc(es_lo, 1)

            def neighbours(b):
                for k in range(TB):
                    n = b * TB + k
                    dve.wait_ge(g_mm, n + 1)
                    own.link(tt(g4[:, k, :], bank(G_BANK[k], D), brow[:, :], ALU.add))
                    tt(gate[:, k, :], ps[:, G_BANK[k], D:D + 2], tile(ex, n)[:, 2:4], ALU.add).then_inc(g_ev, 1)

            def make_gates(b):
                dve.wait_ge(gate_tanh, b + 1)
                ts(gate[:, :, :], gate[:, :, :], 0.5, 0.5, ALU.mult, ALU.add).then_inc(gate_ready, 1)

            def joined(b):
                dve.wait_ge(e_used, (b + 1) * PAIRS)
                own.link(tt(rz[:, :], ps[:, 0:TB, D:D + 1].rearrange("p a b -> p (a b)"),
                            wi[:, bass.ds(b * TB, TB)], ALU.add))
                own.link(nc.vector.reciprocal(rz[:, :], rz[:, :]))
                dve.wait_ge(gate_ready, b + 1)
                own.link(tt(rz[:, :], rz[:, :], gate[:, :, 0], ALU.mult))
                for k in range(TB):
                    n = b * TB + k
                    dve.wait_ge(gated_ready, n + 1)
                    wait_from(dve, sig_ready, n + 1 - TB)
                    stt(z[:, k, :], bank(k, D), rz[:, k:k + 1], g4[:, k, :], ALU.mult, ALU.add) \
                        .then_inc(z_ready, 1)
                dve.wait_ge(z_ready, (b + 1) * TB)

            def residual(b, k):
                n = b * TB + k
                dve.wait_ge(sig_ready, n + 1)
                own.link(tt(y[:, k % 2, :], y[:, k % 2, :], tile(x, n), ALU.add))
                moments(k % 2)
                if k:
                    normed(T + n - 1, (k - 1) % 2, tile(x, n - 1))
                if k == TB - 1:
                    normed(T + n, k % 2, tile(x, n))

            LINKS1 = PAIRS + TB + 3 + 2 * TB

            def block1(b):
                last = isinstance(b, int) and b == B - 1
                for pair in range(2, PAIRS):
                    edge_scores(b, pair)
                    if pair > 2:
                        edge_low(b, pair - 1)
                    if not (isinstance(b, int) and b == 0) and pair - 2 < TB:
                        residual(b - 1, pair - 2)
                    if pair == 6:
                        for f in range(KD):
                            agg_low(0, b, f)
                neighbours(b)
                edge_low(b, PAIRS - 1)
                if not last:
                    edge_scores(b + 1, 0)
                make_gates(b)
                if last:
                    for t in range(4):
                        conv_low(1, t, dsc[:, t:t + 1])
                else:
                    edge_low(b + 1, 0)
                joined(b)
                if not last:
                    edge_scores(b + 1, 1)
                    edge_low(b + 1, 1)

            def conv_low(layer, t, scale):
                dve.wait_ge(conv_hi, layer * T + t + 1)
                stt(x16[:, LO, t, :], x[:, t, :], scale, x16[:, HI, t, :], ALU.mult, ALU.subtract) \
                    .then_inc(conv_lo, 1)

            edge_scores(0, 0)
            edge_scores(0, 1)
            edge_low(0, 0)
            edge_low(0, 1)
            block1(0)
            with dve.Fori(1, B - 1) as b:
                own.enter(b - 1, LINKS1)
                block1(b)
            own.leave(B - 2)
            block1(B - 1)
            for k in range(TB):
                conv_low(1, 4 + 2 * k, dsc[:, 4 + 2 * k:5 + 2 * k])
                conv_low(1, 5 + 2 * k, dsc[:, 5 + 2 * k:6 + 2 * k])
                residual(B - 1, k)
            for t in range(T - TB, T):
                conv_low(1, t, dsc[:, t:t + 1])
            dve.drain().then_inc(l1_done, 1)

            dve.wait_ge(l1_done, 4)
            dve.wait_ge(wt2_landed, 16)
            own.link(nc.vector.tensor_copy(wls[HI][:, :, :], wlf[:, :, :]))
            low(wls[LO][:, :, :], wlf[:, :, :], wls[HI][:, :, :]).then_inc(w_ready, 1)

            def block2(b, between=lambda k: None):
                for k in range(TB):
                    n = b * TB + k
                    dve.wait_ge(relu_ready, TB + n + 1)
                    if k >= 2:
                        normed(2 * T + n - 2, k % 2, tile(x, n - 2))
                    y_free(2 * T + n)
                    tt(y[:, k % 2, :], xb[:, k % 2, :], tile(x, n), ALU.add).then_inc(y2_ready, 1)
                    dve.wait_ge(y2_ready, 2 + n + 1)
                    moments(k % 2)
                    between(k)
                for k in (TB - 2, TB - 1):
                    normed(2 * T + b * TB + k, k % 2, tile(x, b * TB + k))

            agg_low(1, 0, 0)
            with dve.Fori(1, B) as b:
                own.enter(b - 1, TB)
                agg_low(1, b - 1, 1)
                block2(b - 1)
                agg_low(1, b, 0)
            own.leave(B - 1)
            agg_low(1, B - 1, 1)
            block2(B - 1, lambda k: [conv_low(2, t, XS) for t in range(3 * k, 3 * k + 3)])
            for t in range(T - TB, T):
                conv_low(2, t, XS)
            for n, (f, s) in enumerate(((W1f[:, :, :], W1s), (W2f, W2s))):
                dve.wait_ge(wp_hi, n + 1)
                low(s[LO][:, :, :], f, s[HI][:, :, :]).then_inc(wp_ready, 1)
            dve.drain().then_inc(l2_done, 1)

            dve.wait_ge(l2_done, 4)
            def hidden_low(b):
                for o in range(KH):
                    dve.wait_ge(h_f, 2 + b * KH + o + 1)
                    low(hh[LO][:, o, :], hf[:, o % 2, :], hh[HI][:, o, :]).then_inc(h_lo, 1)

            def rows_max(b, of, ahead, first=0):
                for k in range(TB):
                    n = b * TB + k
                    dve.wait_ge(r_copied, 2 + n + 1)
                    nc.vector.tensor_reduce(gm[:, bass.ds(n - first, 1)], tile(of, n - first + ahead), AX_X,
                                            ALU.max, apply_absolute_value=True).then_inc(r_maxed, 1)

            def scales(n):
                nc.vector.reduce_max(g1[:, 0:1], gm[:, :], AX_X).then_inc(tmax_ready, 1)
                dve.wait_ge(gmax_ready, n)
                own.link(ts(g1[:, 3:4], g1[:, 1:2], 1e-30, 1.0 / TOP, ALU.max, ALU.mult))
                nc.vector.reciprocal(g1[:, 2:3], g1[:, 3:4]).then_inc(scale_ready, 1)

            agg_low(2, 0, 0)
            with dve.Fori(1, B) as b:
                agg_low(2, b - 1, 1)
                hidden_low(b - 1)
                rows_max(b - 1, G, AHEAD)
                agg_low(2, b, 0)
            agg_low(2, B - 1, 1)
            hidden_low(B - 1)
            rows_max(B - 1, G, AHEAD)
            dve.wait_ge(r_maxed, T)
            dve.drain().then_inc(h1_done, 1)
            scales(1)
            for t in range(T):
                dve.wait_ge(c3_hi, t + 1)
                stt(g16(t, LO), G[:, t + AHEAD, :], g1[:, 2:3], g16(t, HI), ALU.mult, ALU.subtract) \
                    .then_inc(c3_lo, 1)
            hidden_low(B)
            with dve.Fori(1, B) as b:
                rows_max(B + b - 1, F, 0, T)
                hidden_low(B + b)
            rows_max(2 * B - 1, F, 0, T)
            dve.wait_ge(r_maxed, 2 * T)
            dve.drain().then_inc(h2_done, 1)
            scales(2)
            for t in range(T):
                dve.wait_ge(c3_hi, T + t + 1)
                stt(f16[:, t, D:2 * D], F[:, t, :], g1[:, 2:3], f16[:, t, 0:D], ALU.mult, ALU.subtract) \
                    .then_inc(c3_lo, 1)

            def final3(t, u):
                y_free(3 * T + t)
                dve.wait_ge(o3_mm, t + 1)
                dve.wait_ge(xb_ready, T + t + 1)
                stt(y[:, u, :], bank(u, D), g1[:, 3:4], xb[:, u, :], ALU.mult, ALU.add).then_inc(xb_used, 1)
                dve.wait_ge(xb_used, T + t + 1)
                stt(y[:, u, :], ps[:, u, D:2 * D], g1[:, 3:4], y[:, u, :], ALU.mult, ALU.add).then_inc(o3_read, 1)
                dve.wait_ge(o3_read, t + 1)
                moments(u)

            def store3(t, u, stored):
                wait_from(dve, o_stored[u], 16 * stored)
                normed(3 * T + t, u, ob[:, u, :])

            final3(0, 0)
            final3(1, 1)
            store3(0, 0, 0)

            def pair3(i):
                final3(2 * i, 0)
                store3(2 * i - 1, 1, i - 1)
                final3(2 * i + 1, 1)
                store3(2 * i, 0, i)

            pair3(1)
            with dve.Fori(2, T // 2) as i:
                own.enter(i - 2, 2)
                pair3(i)
            own.leave(T // 2 - 2)
            store3(T - 1, 1, T // 2 - 1)
    return nc


_INS = ['x', 'adj', 'L0_gnn_weight', 'L0_gnn_bias', 'L0_gnn_node_w', 'L0_gnn_edge_w', 'L1_gnn_W_sa', 'L1_gnn_a_sa',
        'L1_gnn_W_gcnb', 'L1_gnn_b_gcnb', 'L1_gnn_Wa', 'L1_gnn_ba', 'L1_gnn_Wb', 'L1_gnn_bb', 'L2_gnn_weight',
        'L3_gnn_W1', 'L3_gnn_b1', 'L3_gnn_W2', 'L3_gnn_b2', 'L3_gnn_W3', 'L3_gnn_b3']


def kernel(**inputs):
    import concourse.bacc as bacc
    from concourse.bass_utils import run_bass_kernel_spmd

    nc = bacc.Bacc("TRN2", target_bir_lowering=False, num_devices=1)
    arrays, args = {}, []
    for name in _INS:
        a = np.ascontiguousarray(inputs[name])
        arrays[f"in_{name}"] = a
        args.append(nc.dram_tensor(f"in_{name}", a.shape, mybir.dt.from_np(a.dtype), kind="ExternalInput").ap())
    out = nc.dram_tensor("out", inputs["x"].shape, F32, kind="ExternalOutput").ap()
    build(nc, *args, out)
    return run_bass_kernel_spmd(nc, [arrays], core_ids=[0]).results[0]["out"]
```
